# Optimizing a Trainium2 kernel written in Bass

```python
import numpy as np
import jax
import jax.numpy as jnp

def _softmax(x, axis=-1):
    return jax.nn.softmax(x, axis=axis)

def _gelu(x):
    return jax.nn.gelu(x, approximate=True)

def _silu(x):
    return jax.nn.silu(x)

def _sigmoid(x):
    return jax.nn.sigmoid(x)

def _layernorm(x, axis=-1, eps=1e-05):
    m = jnp.mean(x, axis=axis, keepdims=True)
    v = jnp.var(x, axis=axis, keepdims=True)
    return (x - m) / jnp.sqrt(v + eps)

def _scatter_add(tgt, idx, src, axis=0):
    return tgt.at[idx].add(src)

def _segment_sum(src, seg, n):
    return jax.ops.segment_sum(src, seg, n)
kernel_name = 'mk_decoder_preln_d2_seqx_r8_1c85c8'

def setup_inputs(seed: int=0):
    np.random.seed(seed)
    _w = jnp.asarray

    def _rec_inputs():
        import jax
        import jax.numpy as jnp
        _rk = jax.random.key(seed)
        x = 0.000341 + 1 * jax.random.normal(jax.random.fold_in(_rk, 1), (16, 128, 256), jnp.float32)
        _lenS = 128 - jax.random.randint(jax.random.fold_in(_rk, 7), (16,), 0, max(1, 128 // 4) + 1, jnp.int32)
        _lenS2 = 128 - jax.random.randint(jax.random.fold_in(_rk, 8), (16,), 0, max(1, 128 // 4) + 1, jnp.int32)
        _ctx_2048P = jax.random.normal(jax.random.fold_in(_rk, 11), (16, 16, 256), jnp.float32)
        _ctx_2048c = jax.random.dirichlet(jax.random.fold_in(_rk, 511), 0.3 * jnp.ones((16,), jnp.float32), (16, 128))
        _ctx_2048t = jnp.einsum('bsk,bkd->bsd', _ctx_2048c, _ctx_2048P)
        _ctx_2048t = _ctx_2048t * jax.lax.rsqrt(jnp.mean(jnp.square(_ctx_2048t)) + 1e-12) * 0.953939
        ctx_2048 = -1.47943e-05 + 1.00017 * (_ctx_2048t + 0.3 * jax.random.normal(jax.random.fold_in(_rk, 611), (16, 128, 256), jnp.float32))
        _validS = jnp.arange(128)[None, :] < _lenS[:, None]
        _validS2 = jnp.arange(128)[None, :] < _lenS2[:, None]
        _causal = jnp.tril(jnp.ones((128, 128), dtype=bool))
        mask_1xSxS2_ff0 = jnp.where(jnp.ones((1, 128, 128), dtype=bool), 0.0, -1000000000.0).astype(jnp.float32)
        return (x, ctx_2048, mask_1xSxS2_ff0)
    x, ctx_2048, mask_1xSxS2_ff0 = _rec_inputs()

    def _L0_attn_setup():
        import jax, jax.numpy as jnp
        import numpy as np
        BATCH, SEQ, D_MODEL, N_HEADS, D_HEAD = (2, 256, 256, 16, 128)
        ATTN_SCALE = np.sqrt(D_HEAD).astype(np.float32)
        IGNORE = jnp.float32(-100000.0)
        key = jax.random.key(seed)
        ks = jax.random.split(key, 5)
        init = 1.0 / np.sqrt(D_MODEL)
        return {'x': jax.random.normal(ks[0], (BATCH, SEQ, D_MODEL), jnp.float32), 'W_Q': jax.random.normal(ks[1], (N_HEADS, D_MODEL, D_HEAD), jnp.float32) * init, 'W_K': jax.random.normal(ks[2], (N_HEADS, D_MODEL, D_HEAD), jnp.float32) * init, 'W_V': jax.random.normal(ks[3], (N_HEADS, D_MODEL, D_HEAD), jnp.float32) * init, 'W_O': jax.random.normal(ks[4], (N_HEADS, D_HEAD, D_MODEL), jnp.float32) * init, 'b_Q': jnp.zeros((N_HEADS, D_HEAD), jnp.float32), 'b_K': jnp.zeros((N_HEADS, D_HEAD), jnp.float32), 'b_V': jnp.zeros((N_HEADS, D_HEAD), jnp.float32), 'b_O': jnp.zeros((D_MODEL,), jnp.float32)}
    _L0_attn_all = _L0_attn_setup()
    _L0_attn_in = {k: v for k, v in _L0_attn_all.items() if k in ('W_Q', 'W_K', 'W_V', 'W_O', 'b_Q', 'b_K', 'b_V', 'b_O')}
    del _L0_attn_all

    def _L0_xattn_setup():
        import jax, jax.numpy as jnp
        import numpy as np

        def _wkv(time_decay, time_first, k, v):
            w = -jnp.exp(time_decay)
            u = time_first
            B, T, C = k.shape
            aa = jnp.zeros((B, C), dtype=k.dtype)
            bb = jnp.zeros((B, C), dtype=k.dtype)
            pp = jnp.full((B, C), -1e+38, dtype=k.dtype)

            def step(carry, kv_t):
                aa, bb, pp = carry
                kt, vt = kv_t
                ww = u + kt
                q = jnp.maximum(pp, ww)
                e1 = jnp.exp(pp - q)
                e2 = jnp.exp(ww - q)
                y_t = (e1 * aa + e2 * vt) / (e1 * bb + e2)
                ww2 = pp + w
                q2 = jnp.maximum(ww2, kt)
                e1b = jnp.exp(ww2 - q2)
                e2b = jnp.exp(kt - q2)
                new_carry = (e1b * aa + e2b * vt, e1b * bb + e2b, q2)
                return (new_carry, y_t)
            ks = jnp.transpose(k, (1, 0, 2))
            vs = jnp.transpose(v, (1, 0, 2))
            _, ys = jax.lax.scan(step, (aa, bb, pp), (ks, vs))
            return jnp.transpose(ys, (1, 0, 2))
        key = jax.random.key(seed)
        k1, k2, k3, k4 = jax.random.split(key, 4)
        B, T, C = (8, 128, 256)
        return {'batch_size': B, 'seq_len': T, 'embedding_dim': C, 'time_decay': jax.random.normal(k1, (C,), dtype=jnp.float32), 'time_first': jax.random.normal(k2, (C,), dtype=jnp.float32), 'k': jax.random.normal(k3, (B, T, C), dtype=jnp.float32), 'v': jax.random.normal(k4, (B, T, C), dtype=jnp.float32)}
    _L0_xattn_all = _L0_xattn_setup()
    _L0_xattn_in = {k: v for k, v in _L0_xattn_all.items() if k in ('time_decay', 'time_first')}
    del _L0_xattn_all

    def _L0_ffn_setup():
        import jax, jax.numpy as jnp
        import numpy as np
        B, S, H = (2, 256, 256)
        E, K = (16, 4)
        I_MOE, I_SH = (176, 704)
        key = jax.random.key(seed)
        ks = jax.random.split(key, 9)

        def w(k, shape, fan_in):
            return jax.random.normal(k, shape, jnp.float32) * fan_in ** (-0.5)
        return {'hidden_states': jax.random.normal(ks[0], (B, S, H), jnp.float32), 'router_w': w(ks[1], (E, H), H), 'w_gate': w(ks[2], (E, H, I_MOE), H), 'w_up': w(ks[3], (E, H, I_MOE), H), 'w_down': w(ks[4], (E, I_MOE, H), I_MOE), 'sh_gate': w(ks[5], (H, I_SH), H), 'sh_up': w(ks[6], (H, I_SH), H), 'sh_down': w(ks[7], (I_SH, H), I_SH), 'sh_gate_w': w(ks[8], (H, 1), H)}
    _L0_ffn_all = _L0_ffn_setup()
    _L0_ffn_in = {k: v for k, v in _L0_ffn_all.items() if k in ('router_w', 'w_gate', 'w_up', 'w_down', 'sh_gate', 'sh_up', 'sh_down', 'sh_gate_w')}
    del _L0_ffn_all

    def _L1_attn_setup():
        import jax, jax.numpy as jnp
        import numpy as np
        DIMS = 256
        HEAD = 16
        HD = DIMS // HEAD
        EPS = float(np.finfo(np.float32).eps)

        def _rms(x, g):
            return x * jax.lax.rsqrt(jnp.mean(x * x, axis=-1, keepdims=True) + EPS) * g
        key = jax.random.key(seed)
        ks = jax.random.split(key, 8)
        B, T, D = (2, 256, DIMS)
        s = 1.0 / np.sqrt(D)
        return {'x': jax.random.normal(ks[0], (B, T, D), dtype=jnp.float32), 'g_q': jnp.ones((D,), jnp.float32), 'Wq': jax.random.normal(ks[1], (D, D), jnp.float32) * s, 'bq': jnp.zeros((D,), jnp.float32), 'g_kv': jnp.ones((D,), jnp.float32), 'Wkv': jax.random.normal(ks[2], (D, 2 * D), jnp.float32) * s, 'bkv': jnp.zeros((2 * D,), jnp.float32), 'g_head': jnp.ones((HD,), jnp.float32), 'Wo': jax.random.normal(ks[3], (D, D), jnp.float32) * s, 'bo': jnp.zeros((D,), jnp.float32)}
    _L1_attn_all = _L1_attn_setup()
    _L1_attn_in = {k: v for k, v in _L1_attn_all.items() if k in ('g_q', 'Wq', 'bq', 'g_kv', 'Wkv', 'bkv', 'g_head', 'Wo', 'bo')}
    del _L1_attn_all

    def _L1_xattn_setup():
        import jax, jax.numpy as jnp
        import numpy as np
        H = 256
        NH = 16
        NKV = 4
        HD = 128
        GROUPS = NH // NKV
        EPS = 1e-06
        B, S, SE = (1, 256, 512)

        def _rmsnorm(x, w, eps=EPS):
            xf = x.astype(jnp.float32)
            var = jnp.mean(xf * xf, axis=-1, keepdims=True)
            return (xf * jax.lax.rsqrt(var + eps)).astype(x.dtype) * w
        key = jax.random.key(seed)
        ks = jax.random.split(key, 12)
        sc = 0.02
        return {'hidden_states': jax.random.normal(ks[0], (B, S, H), jnp.float32), 'encoder_hidden_states': jax.random.normal(ks[1], (B, SE, H), jnp.float32), 'attention_mask': jnp.zeros((B, S, SE), jnp.float32), 'Wq': jax.random.normal(ks[2], (H, NH * HD), jnp.float32) * sc, 'bq': jax.random.normal(ks[3], (NH * HD,), jnp.float32) * sc, 'Wk': jax.random.normal(ks[4], (H, NKV * HD), jnp.float32) * sc, 'bk': jax.random.normal(ks[5], (NKV * HD,), jnp.float32) * sc, 'Wv': jax.random.normal(ks[6], (H, NKV * HD), jnp.float32) * sc, 'bv': jax.random.normal(ks[7], (NKV * HD,), jnp.float32) * sc, 'Wo': jax.random.normal(ks[8], (NH * HD, H), jnp.float32) * sc, 'qn_w': jnp.ones((HD,), jnp.float32), 'kn_w': jnp.ones((HD,), jnp.float32)}
    _L1_xattn_all = _L1_xattn_setup()
    _L1_xattn_in = {k: v for k, v in _L1_xattn_all.items() if k in ('Wq', 'bq', 'Wk', 'bk', 'Wv', 'bv', 'Wo', 'qn_w', 'kn_w')}
    del _L1_xattn_all

    def _L1_ffn_setup():
        import jax, jax.numpy as jnp
        import numpy as np
        EPS = 1e-05

        def weight_quant(w):
            scale = 1.0 / jnp.clip(jnp.mean(jnp.abs(w)), EPS, None)
            return jnp.clip(jnp.round(w * scale), -1.0, 1.0) / scale

        def act_quant(x):
            scale = 127.0 / jnp.clip(jnp.max(jnp.abs(x), axis=-1, keepdims=True), EPS, None)
            return jnp.clip(jnp.round(x * scale), -128.0, 127.0) / scale

        def bitlinear(x, w):
            return jnp.einsum('bsd,od->bso', act_quant(x), weight_quant(w))
        key = jax.random.key(seed)
        k1, k2, k3, k4 = jax.random.split(key, 4)
        B, S, D = (4, 256, 256)
        I = int(np.ceil(D * np.pi / 64) * 64)
        x = jax.random.normal(k1, (B, S, D), dtype=jnp.float32)
        w_gate = jax.random.normal(k2, (I, D), dtype=jnp.float32) * 0.02
        w_up = jax.random.normal(k3, (I, D), dtype=jnp.float32) * 0.02
        w_down = jax.random.normal(k4, (D, I), dtype=jnp.float32) * 0.02
        return {'x': x, 'w_gate': w_gate, 'w_up': w_up, 'w_down': w_down}
    _L1_ffn_all = _L1_ffn_setup()
    _L1_ffn_in = {k: v for k, v in _L1_ffn_all.items() if k in ('w_gate', 'w_up', 'w_down')}
    del _L1_ffn_all
    return {'x': x, 'ctx_2048': ctx_2048, 'mask_1xSxS2_ff0': mask_1xSxS2_ff0, 'L0_attn_W_Q': _L0_attn_in['W_Q'], 'L0_attn_W_K': _L0_attn_in['W_K'], 'L0_attn_W_V': _L0_attn_in['W_V'], 'L0_attn_W_O': _L0_attn_in['W_O'], 'L0_attn_b_Q': _L0_attn_in['b_Q'], 'L0_attn_b_K': _L0_attn_in['b_K'], 'L0_attn_b_V': _L0_attn_in['b_V'], 'L0_attn_b_O': _L0_attn_in['b_O'], 'L0_xattn_time_decay': _L0_xattn_in['time_decay'], 'L0_xattn_time_first': _L0_xattn_in['time_first'], 'L0_ffn_router_w': _L0_ffn_in['router_w'], 'L0_ffn_w_gate': _L0_ffn_in['w_gate'], 'L0_ffn_w_up': _L0_ffn_in['w_up'], 'L0_ffn_w_down': _L0_ffn_in['w_down'], 'L0_ffn_sh_gate': _L0_ffn_in['sh_gate'], 'L0_ffn_sh_up': _L0_ffn_in['sh_up'], 'L0_ffn_sh_down': _L0_ffn_in['sh_down'], 'L0_ffn_sh_gate_w': _L0_ffn_in['sh_gate_w'], 'L1_attn_g_q': _L1_attn_in['g_q'], 'L1_attn_Wq': _L1_attn_in['Wq'], 'L1_attn_bq': _L1_attn_in['bq'], 'L1_attn_g_kv': _L1_attn_in['g_kv'], 'L1_attn_Wkv': _L1_attn_in['Wkv'], 'L1_attn_bkv': _L1_attn_in['bkv'], 'L1_attn_g_head': _L1_attn_in['g_head'], 'L1_attn_Wo': _L1_attn_in['Wo'], 'L1_attn_bo': _L1_attn_in['bo'], 'L1_xattn_Wq': _L1_xattn_in['Wq'], 'L1_xattn_bq': _L1_xattn_in['bq'], 'L1_xattn_Wk': _L1_xattn_in['Wk'], 'L1_xattn_bk': _L1_xattn_in['bk'], 'L1_xattn_Wv': _L1_xattn_in['Wv'], 'L1_xattn_bv': _L1_xattn_in['bv'], 'L1_xattn_Wo': _L1_xattn_in['Wo'], 'L1_xattn_qn_w': _L1_xattn_in['qn_w'], 'L1_xattn_kn_w': _L1_xattn_in['kn_w'], 'L1_ffn_w_gate': _L1_ffn_in['w_gate'], 'L1_ffn_w_up': _L1_ffn_in['w_up'], 'L1_ffn_w_down': _L1_ffn_in['w_down']}

def reference(x, ctx_2048, mask_1xSxS2_ff0, L0_attn_W_Q, L0_attn_W_K, L0_attn_W_V, L0_attn_W_O, L0_attn_b_Q, L0_attn_b_K, L0_attn_b_V, L0_attn_b_O, L0_xattn_time_decay, L0_xattn_time_first, L0_ffn_router_w, L0_ffn_w_gate, L0_ffn_w_up, L0_ffn_w_down, L0_ffn_sh_gate, L0_ffn_sh_up, L0_ffn_sh_down, L0_ffn_sh_gate_w, L1_attn_g_q, L1_attn_Wq, L1_attn_bq, L1_attn_g_kv, L1_attn_Wkv, L1_attn_bkv, L1_attn_g_head, L1_attn_Wo, L1_attn_bo, L1_xattn_Wq, L1_xattn_bq, L1_xattn_Wk, L1_xattn_bk, L1_xattn_Wv, L1_xattn_bv, L1_xattn_Wo, L1_xattn_qn_w, L1_xattn_kn_w, L1_ffn_w_gate, L1_ffn_w_up, L1_ffn_w_down):
    import jax
    import jax.numpy as jnp

    def _L0_attn_ref(x, W_Q, W_K, W_V, W_O, b_Q, b_K, b_V, b_O):
        import jax, jax.numpy as jnp
        import numpy as np
        BATCH, SEQ, D_MODEL, N_HEADS, D_HEAD = (2, 256, 256, 16, 128)
        ATTN_SCALE = np.sqrt(D_HEAD).astype(np.float32)
        IGNORE = jnp.float32(-100000.0)
        q = jnp.einsum('bpd,hde->bphe', x, W_Q) + b_Q
        k = jnp.einsum('bpd,hde->bphe', x, W_K) + b_K
        v = jnp.einsum('bpd,hde->bphe', x, W_V) + b_V
        scores = jnp.einsum('bqhe,bkhe->bhqk', q, k) / ATTN_SCALE
        S = x.shape[1]
        causal = jnp.tril(jnp.ones((S, S), bool))
        scores = jnp.where(causal, scores, IGNORE)
        attn = jax.nn.softmax(scores, axis=-1)
        z = jnp.einsum('bkhe,bhqk->bqhe', v, attn)
        out = jnp.einsum('bqhe,hed->bqd', z, W_O) + b_O
        return out

    def _L0_xattn_ref(batch_size, seq_len, embedding_dim, time_decay, time_first, k, v):
        import jax, jax.numpy as jnp
        import numpy as np

        def _wkv(time_decay, time_first, k, v):
            w = -jnp.exp(time_decay)
            u = time_first
            B, T, C = k.shape
            aa = jnp.zeros((B, C), dtype=k.dtype)
            bb = jnp.zeros((B, C), dtype=k.dtype)
            pp = jnp.full((B, C), -1e+38, dtype=k.dtype)

            def step(carry, kv_t):
                aa, bb, pp = carry
                kt, vt = kv_t
                ww = u + kt
                q = jnp.maximum(pp, ww)
                e1 = jnp.exp(pp - q)
                e2 = jnp.exp(ww - q)
                y_t = (e1 * aa + e2 * vt) / (e1 * bb + e2)
                ww2 = pp + w
                q2 = jnp.maximum(ww2, kt)
                e1b = jnp.exp(ww2 - q2)
                e2b = jnp.exp(kt - q2)
                new_carry = (e1b * aa + e2b * vt, e1b * bb + e2b, q2)
                return (new_carry, y_t)
            ks = jnp.transpose(k, (1, 0, 2))
            vs = jnp.transpose(v, (1, 0, 2))
            _, ys = jax.lax.scan(step, (aa, bb, pp), (ks, vs))
            return jnp.transpose(ys, (1, 0, 2))
        assert seq_len <= 128
        return _wkv(time_decay, time_first, k, v)

    def _L0_ffn_ref(hidden_states, router_w, w_gate, w_up, w_down, sh_gate, sh_up, sh_down, sh_gate_w):
        import jax, jax.numpy as jnp
        import numpy as np
        B, S, H = (2, 256, 256)
        E, K = (16, 4)
        I_MOE, I_SH = (176, 704)
        orig = hidden_states.shape
        h = hidden_states.reshape(-1, orig[-1])
        N = h.shape[0]
        logits = h @ router_w.T
        probs = jax.nn.softmax(logits.astype(jnp.float32), axis=-1)
        top_vals, top_idx = jax.lax.top_k(probs, K)
        top_vals = top_vals / jnp.maximum(top_vals.sum(-1, keepdims=True), 1e-09)
        top_vals = top_vals.astype(h.dtype)
        comb = jnp.zeros((N, E), h.dtype).at[jnp.arange(N)[:, None], top_idx].add(top_vals)
        g = jnp.einsum('nh,ehi->eni', h, w_gate)
        u = jnp.einsum('nh,ehi->eni', h, w_up)
        y = jnp.einsum('eni,eih->enh', jax.nn.silu(g) * u, w_down)
        routed = jnp.einsum('enh,ne->nh', y, comb)
        shared = jax.nn.silu(h @ sh_gate) * (h @ sh_up) @ sh_down
        sg = jax.nn.sigmoid(h @ sh_gate_w)
        return (routed + sg * shared).reshape(orig)

    def _L1_attn_ref(x, g_q, Wq, bq, g_kv, Wkv, bkv, g_head, Wo, bo):
        import jax, jax.numpy as jnp
        import numpy as np
        DIMS = 256
        HEAD = 16
        HD = DIMS // HEAD
        EPS = float(np.finfo(np.float32).eps)

        def _rms(x, g):
            return x * jax.lax.rsqrt(jnp.mean(x * x, axis=-1, keepdims=True) + EPS) * g
        B, T, D = x.shape
        H, d = (HEAD, HD)
        q = (_rms(x, g_q) @ Wq + bq).reshape(B, T, H, d).transpose(0, 2, 1, 3)
        kv = (_rms(x, g_kv) @ Wkv + bkv).reshape(B, T, 2, H, d)
        k = kv[:, :, 0].transpose(0, 2, 1, 3)
        v = kv[:, :, 1].transpose(0, 2, 1, 3)
        scale = d ** (-0.5)
        scores = jnp.einsum('bhqd,bhkd->bhqk', _rms(q, g_head), _rms(k, g_head)) * scale
        attn = jax.nn.softmax(scores, axis=-1)
        wv = jnp.einsum('bhqk,bhkd->bhqd', attn, v)
        out = wv.transpose(0, 2, 1, 3).reshape(B, T, D) @ Wo + bo
        return out

    def _L1_xattn_ref(hidden_states, encoder_hidden_states, attention_mask, Wq, bq, Wk, bk, Wv, bv, Wo, qn_w, kn_w):
        import jax, jax.numpy as jnp
        import numpy as np
        H = 256
        NH = 16
        NKV = 4
        HD = 128
        GROUPS = NH // NKV
        EPS = 1e-06
        B, S, SE = (1, 256, 512)

        def _rmsnorm(x, w, eps=EPS):
            xf = x.astype(jnp.float32)
            var = jnp.mean(xf * xf, axis=-1, keepdims=True)
            return (xf * jax.lax.rsqrt(var + eps)).astype(x.dtype) * w
        b, s, _ = hidden_states.shape
        se = encoder_hidden_states.shape[1]
        q = (hidden_states @ Wq + bq).reshape(b, s, NH, HD).transpose(0, 2, 1, 3)
        k = (encoder_hidden_states @ Wk + bk).reshape(b, se, NKV, HD).transpose(0, 2, 1, 3)
        v = (encoder_hidden_states @ Wv + bv).reshape(b, se, NKV, HD).transpose(0, 2, 1, 3)
        k = jnp.repeat(k, GROUPS, axis=1)
        v = jnp.repeat(v, GROUPS, axis=1)
        q = _rmsnorm(q, qn_w)
        k = _rmsnorm(k, kn_w)
        scale = 1.0 / np.sqrt(HD).astype(np.float32)
        scores = jnp.einsum('bhsd,bhed->bhse', q, k) * scale
        scores = scores + attention_mask[:, None, :, :]
        probs = jax.nn.softmax(scores.astype(jnp.float32), axis=-1).astype(q.dtype)
        out = jnp.einsum('bhse,bhed->bhsd', probs, v)
        out = out.transpose(0, 2, 1, 3).reshape(b, s, NH * HD)
        return out @ Wo

    def _L1_ffn_ref(x, w_gate, w_up, w_down):
        import jax, jax.numpy as jnp
        import numpy as np
        EPS = 1e-05

        def weight_quant(w):
            scale = 1.0 / jnp.clip(jnp.mean(jnp.abs(w)), EPS, None)
            return jnp.clip(jnp.round(w * scale), -1.0, 1.0) / scale

        def act_quant(x):
            scale = 127.0 / jnp.clip(jnp.max(jnp.abs(x), axis=-1, keepdims=True), EPS, None)
            return jnp.clip(jnp.round(x * scale), -128.0, 127.0) / scale

        def bitlinear(x, w):
            return jnp.einsum('bsd,od->bso', act_quant(x), weight_quant(w))
        gate = jax.nn.silu(bitlinear(x, w_gate))
        up = bitlinear(x, w_up)
        return bitlinear(gate * up, w_down)
    x = x + _L0_attn_ref(_layernorm(x, axis=-1), L0_attn_W_Q, L0_attn_W_K, L0_attn_W_V, L0_attn_W_O, L0_attn_b_Q, L0_attn_b_K, L0_attn_b_V, L0_attn_b_O)
    x = x + _L0_xattn_ref(16, 128, 256, L0_xattn_time_decay, L0_xattn_time_first, _layernorm(x, axis=-1), ctx_2048)
    x = x + _L0_ffn_ref(_layernorm(x, axis=-1), L0_ffn_router_w, L0_ffn_w_gate, L0_ffn_w_up, L0_ffn_w_down, L0_ffn_sh_gate, L0_ffn_sh_up, L0_ffn_sh_down, L0_ffn_sh_gate_w)
    x = x + _L1_attn_ref(_layernorm(x, axis=-1), L1_attn_g_q, L1_attn_Wq, L1_attn_bq, L1_attn_g_kv, L1_attn_Wkv, L1_attn_bkv, L1_attn_g_head, L1_attn_Wo, L1_attn_bo)
    x = x + _L1_xattn_ref(_layernorm(x, axis=-1), ctx_2048, mask_1xSxS2_ff0, L1_xattn_Wq, L1_xattn_bq, L1_xattn_Wk, L1_xattn_bk, L1_xattn_Wv, L1_xattn_bv, L1_xattn_Wo, L1_xattn_qn_w, L1_xattn_kn_w)
    x = x + _L1_ffn_ref(_layernorm(x, axis=-1), L1_ffn_w_gate, L1_ffn_w_up, L1_ffn_w_down)
    return x

_drawn_inputs = setup_inputs


def setup_inputs(seed=0):
    import zlib

    import numpy as np

    out = dict(_drawn_inputs(seed))
    spreads = {'L0_attn_b_Q': (0.0, 0.1),
     'L0_attn_b_K': (0.0, 0.8),
     'L0_attn_b_V': (0.0, 0.1),
     'L0_attn_b_O': (0.0, 0.1),
     'L1_attn_g_q': (1.0, 0.6),
     'L1_attn_bq': (0.0, 0.712),
     'L1_attn_g_kv': (1.0, 0.2),
     'L1_attn_bkv': (0.0, 0.1),
     'L1_attn_g_head': (1.0, 0.2),
     'L1_attn_bo': (0.0, 0.1),
     'L1_xattn_qn_w': (1.0, 0.6),
     'L1_xattn_kn_w': (1.0, 0.6)}
    factors = {'L1_xattn_bq': 8.0,
     'L1_xattn_bk': 8.0,
     'L1_xattn_bv': 5.472,
     'L1_ffn_w_gate': 8.0,
     'L1_ffn_w_up': 8.0,
     'L1_ffn_w_down': 8.0}
    for name, (base, spread) in spreads.items():
        noise = np.random.default_rng([zlib.crc32(name.encode()), seed]).standard_normal(out[name].shape)
        drawn = base * np.exp(spread * noise) if base else spread * noise
        out[name] = jnp.asarray(drawn.astype(out[name].dtype))
    for name, factor in factors.items():
        out[name] = (out[name] * factor).astype(out[name].dtype)
    return out
```

```python
from contextlib import ExitStack

import numpy as np

import concourse.bass as bass
from concourse import mybir

F32 = mybir.dt.float32
F32R = mybir.dt.float32r
BF16 = mybir.dt.bfloat16
ALU = mybir.AluOpType
ACT = mybir.ActivationFunctionType
AX = mybir.AxisListType

P = 128
B = 16
D = 256
KT = D // P
GB = 4
NG = B // GB
GT = GB * P
NT = B * P
H = 16
HG = 4
NHG = H // HG
DH = 128
DS = D // H
NKV = 4
E = 16
EI = 176
SI = 704
TOPK = 4
HID = E * EI + SI
NJ = -(-HID // P)
JW = 6 * P
BI = 832
BJ = -(-BI // P)
NSPLIT = 3
CW = E + 1
ROUND = 12582912.0
LN_EPS = 1e-5
RMS_EPS = float(np.finfo(np.float32).eps)
QK_EPS = 1e-6
PHASE_COLUMNS = 39600
NEG = -1e30
SEG = P + 1


class Signal:

    def __init__(self, sem):
        self.sem, self.count = sem, 0


class Queue:

    def __init__(self, wait_ge, own):
        self.steps, self.passed, self.wait_ge, self.own = [], {}, wait_ge, own
        self.mark = None

    def wait(self, *marks):
        for m in marks:
            if m is not None and self.passed.get(m[0], 0) < m[1]:
                self.passed[m[0]] = m[1]
                self.steps.append((self.wait_ge, (m[0].sem, m[1]), {}, None, 0))

    def do(self, method, *args, signal=None, by=1, **kw):
        signal = signal or self.own
        signal.count += by
        self.steps.append((method, args, kw, signal.sem, by))
        if by == 1:
            self.mark = (signal, signal.count)
        return (signal, signal.count)

    def quiet(self, method, *args, **kw):
        self.steps.append((method, args, kw, None, 0))

    def emit(self):
        for method, args, kw, sem, by in self.steps:
            made = method(*args, **kw)
            if sem is not None:
                made.then_inc(sem, by)


class Bank:

    def __init__(self, tensor):
        self.t, self.free = tensor, None


def build(nc, io, out, phases=6):
    with ExitStack() as ctx:
        def sb(name, shape, dt=F32):
            return ctx.enter_context(nc.sbuf_tensor(name, shape, dt))

        def signal(name):
            return Signal(ctx.enter_context(nc.semaphore(name)))

        pe = Queue(nc.tensor.wait_ge, signal("pe_steps"))
        dve = Queue(nc.vector.wait_ge, signal("dve_steps"))
        act = Queue(nc.scalar.wait_ge, signal("act_steps"))
        pool = Queue(nc.gpsimd.wait_ge, signal("pool_steps"))
        sp = Queue(nc.sync.wait_ge, signal("sp_unused"))
        V, S, G, T = nc.vector, nc.scalar, nc.gpsimd, nc.tensor

        def load(name, dst, src):
            return sp.do(nc.sync.dma_start, dst, src, signal=signal(name), by=16)

        def phase_end():
            marks = [q.mark for q in (pe, dve, act, pool)]
            for q in (pe, dve, act, pool, sp):
                q.wait(*marks)

        X = sb("residual", [P, B, D])
        XT = sb("x_channel_major", [P, 2, KT, NT], F32R)
        ident = sb("identity", [P, P])
        identb = sb("identity_bf16", [P, P], BF16)
        vec = sb("channel_vectors", [P, 64])
        small = sb("small", [P, 1024])
        banks = [Bank(ctx.enter_context(nc.psum_tensor(f"bank{i}", [P, 512], F32))) for i in range(8)]

        class Carve:

            def __init__(self, t, width):
                self.t, self.width, self.at = t, width, 0

            def take(self, n):
                n += n % 2
                a = self.t[:, self.at:self.at + n]
                self.at += n
                assert self.at <= self.width, (self.at, self.width)
                return a

        got_x = []
        got_x.append(load("load_x0", X[:, 0:GB, :], io["x"][:, 0:GB, :]))
        got_id = load("load_ident", ident[:, :], io["ident"])
        got_idb = load("load_identb", identb[:, :], io["identb"])
        got_vec = load("load_vec", vec[:, :], io["vec"])
        for g in range(1, NG):
            got_x.append(load(f"load_x{g}", X[:, g * GB:(g + 1) * GB, :], io["x"][:, g * GB:(g + 1) * GB, :]))
        x_ready = list(got_x)

        def phase_memory(name, scope, n_split, n_plain=None):
            n_plain = n_plain or PHASE_COLUMNS - n_split
            parts = []
            if n_split:
                t = scope.enter_context(nc.sbuf_tensor(f"{name}_split", [P, n_split], F32R))
                parts.append(Carve(t, n_split))
            t = scope.enter_context(nc.sbuf_tensor(f"{name}_plain", [P, n_plain], F32))
            return *parts, Carve(t, n_plain)

        sm = Carve(small, 1024)
        eps_ln, eps_rms, eps_qk, eps_both = (sm.take(2) for _ in range(4))
        dve.do(V.memset, eps_ln[:, 0:1], LN_EPS)
        dve.do(V.memset, eps_rms[:, 0:1], RMS_EPS)
        dve.do(V.memset, eps_both[:, 0:1], RMS_EPS * LN_EPS)
        got_eps = dve.do(V.memset, eps_qk[:, 0:1], QK_EPS)
        stats = sm.take(GB * 6 * 2).rearrange("p (s b c) -> p s b c", s=2, b=GB)
        mv = sm.take(GB * 2 * 2).rearrange("p (s b c) -> p s b c", s=2, b=GB)
        sd = sm.take(GB * 2).rearrange("p (s b) -> p s b", s=2)
        rstd = sm.take(GB * 2).rearrange("p (s b) -> p s b", s=2)
        small_base = sm.at

        def matmul3(out_ap, w_hi, w_lo, x_hi, x_lo, first, last):
            pe.quiet(T.matmul, out_ap, w_hi, x_hi, start=first, stop=False)
            pe.quiet(T.matmul, out_ap, w_hi, x_lo, start=False, stop=False)
            if last:
                return pe.do(T.matmul, out_ap, w_lo, x_hi, start=False, stop=True)
            pe.quiet(T.matmul, out_ap, w_lo, x_hi, start=False, stop=False)

        def project(bank, pairs):
            pe.wait(bank.free)
            m = None
            for i, (w_hi, w_lo, x_hi, x_lo) in enumerate(pairs):
                m = matmul3(bank.t[:, 0:x_hi.shape[-1]], w_hi, w_lo, x_hi, x_lo, i == 0, i == len(pairs) - 1)
            return m

        def split(hi, lo, src, ready, hi_q, hi_op, lo_q, lo_op, kw=None):
            hi_q.wait(*ready)
            a = hi_q.do(hi_op, hi, src, **(kw or {}))
            lo_q.wait(a, *ready)
            return lo_q.do(lo_op, lo, src, hi.bitcast(F32), ALU.subtract)

        xn_free = [None] * 8
        sd_ready = {}

        def moments(g, then_rms=False):
            s = g % 2
            dve.wait(x_ready[g])
            for b in range(GB):
                m = dve.do(V.bn_stats, stats[:, s, b, :], X[:, g * GB + b, :])
            dve.wait(m)
            for b in range(GB):
                m = dve.do(V.bn_aggr, mv[:, s, b, :], stats[:, s, b, :])
            act.wait(m, got_eps)
            eps, scale = (eps_both, 1.0 + RMS_EPS) if then_rms else (eps_ln, 1.0)
            sd_ready[g] = act.do(S.activation, sd[:, s, :], mv[:, s, :, 1], ACT.Sqrt, bias=eps[:, 0:1], scale=scale)

        def normalised(g, xn):
            s = g % 2
            dve.wait(sd_ready[g])
            m = dve.do(V.reciprocal, rstd[:, s, :], sd[:, s, :])
            dve.wait(m)
            marks = []
            for b in range(GB):
                dve.wait(xn_free[s * GB + b])
                marks.append(dve.do(V.tensor_scalar, xn[s][:, b, :], X[:, g * GB + b, :], mv[:, s, b, 0:1],
                                    rstd[:, s, b:b + 1], ALU.subtract, ALU.mult))
            return marks

        def to_channels(g, xn, marks, kt, bank):
            s = g % 2
            pe.wait(bank.free, got_id)
            for b in range(GB):
                pe.wait(marks[b])
                m = pe.do(T.transpose, bank.t[:, b * P:(b + 1) * P], xn[s][:, b, kt * P:(kt + 1) * P],
                          ident[:, :])
                if kt == KT - 1:
                    xn_free[s * GB + b] = m
            return m

        def split_channels(g, xn, marks, kt, bank):
            done = to_channels(g, xn, marks, kt, bank)
            sl = slice(g * GT, (g + 1) * GT)
            bank.free = split(XT[:, 0, kt, sl], XT[:, 1, kt, sl], bank.t[:, :], [done],
                              act, S.copy, dve, V.tensor_tensor)
            return bank.free

        def norm_to_xt(g, xn, two_banks):
            marks = normalised(g, xn)
            for kt in range(KT):
                m = split_channels(g, xn, marks, kt, two_banks[kt])
            return m

        def norm_all_to_xt(xn, bank_pairs):
            ready = []
            moments(0)
            for g in range(NG):
                if g + 1 < NG:
                    moments(g + 1)
                ready.append(norm_to_xt(g, xn, bank_pairs[g % len(bank_pairs)]))
            return ready

        def four(ap):
            return ap.rearrange("p (h k) -> p h k", h=HG)

        def row_max(negmax, scores_in, ready):
            dve.wait(ready)
            return dve.do(V.tensor_reduce, negmax, scores_in, AX.X, ALU.max, negate=True)

        def exponentials(probs, scores_in, negmax, sums, ready, free):
            act.wait(ready, free)
            for h in range(HG):
                m = act.do(S.activation, probs[:, h, :], scores_in[:, h, :], ACT.Exp, bias=negmax[:, h:h + 1],
                           accum_out=sums[:, h:h + 1])
            return m

        def normalise(probs, sums, rinv, ready):
            dve.wait(ready)
            m = dve.do(V.reciprocal, rinv, sums)
            dve.wait(m)
            return dve.do(V.tensor_tensor, probs, probs, rinv.unsqueeze(2).broadcast_to([P, HG, P]), ALU.mult)

        def phase1(scope):
            wr, ar = phase_memory("self_attention", scope, 12288)
            raw = ar.take(3 * KT * HG * DH)
            wo = [ar.take(HG * D).rearrange("p (h d) -> p h d", h=HG) for _ in range(2)]
            qT = [ar.take(HG * GT).rearrange("p (h t) -> p h t", h=HG) for _ in range(2)]
            kT = [ar.take(HG * GT).rearrange("p (h t) -> p h t", h=HG) for _ in range(2)]
            vv = [ar.take(GB * HG * DH).rearrange("p (b c) -> p b c", b=GB) for _ in range(2)]
            Smask = [ar.take(512).rearrange("p (h k) -> p h k", h=HG) for _ in range(2)]
            Pm = [ar.take(512).rearrange("p (h k) -> p h k", h=HG) for _ in range(2)]
            PT = [ar.take(512).rearrange("p (h k) -> p h k", h=HG) for _ in range(2)]
            ZT = [ar.take(512).rearrange("p (h k) -> p h k", h=HG) for _ in range(2)]
            bvb = ar.take(H * DH)
            xn = [ar.take(GB * D).rearrange("p (b d) -> p b d", b=GB) for _ in range(2)]
            bob = ar.take(D)
            causal = ar.take(P)
            sm.at = small_base
            negmax = [sm.take(HG) for _ in range(2)]
            sums = [sm.take(HG) for _ in range(2)]
            rinv = [sm.take(HG) for _ in range(2)]
            bqs = sm.take(H)
            scale = 1.0 / float(np.sqrt(np.float32(DH)))

            WS = 3 * KT * HG * DH
            wr = [[wr.take(WS).rearrange("p (m k c) -> p m k c", m=3, k=KT) for part in range(2)]
                  for s in range(2)]
            raw_v = raw.rearrange("p (m k c) -> p m k c", m=3, k=KT)

            weights_ready, wo_ready = {}, {}
            raw_free = [None]
            wr_free = [None, None]
            wo_free = [None, None]

            def fetch_weights(hg):
                s = hg % 2
                sp.wait(raw_free[0], wo_free[s])
                got = load(f"load_wqkv{hg}", raw, io["wqkv0"][:, hg])
                wo_ready[hg] = load(f"load_wo{hg}", wo[s], io["wo0"][:, hg])
                marks = []
                for m in range(3):
                    hq, hop, lq, lop = (act, S.copy, dve, V.tensor_tensor) if hg == 0 else \
                                       (pool, G.tensor_copy, pool, G.tensor_tensor)
                    marks.append(split(wr[s][0][:, m], wr[s][1][:, m], raw_v[:, m], [got, wr_free[s]],
                                       hq, hop, lq, lop))
                weights_ready[hg] = marks
                raw_free[0] = marks[-1]

            got_causal = load("load_causal", causal, io["causal"])
            fetch_weights(0)
            got_bv = load("load_bv", bvb, io["bv0"].partition_broadcast(P))
            got_bo = load("load_bo", bob, io["bo0"].partition_broadcast(P))
            act.wait(got_vec)
            got_bqs = act.do(S.mul, bqs, vec[:, 0:H], scale)

            xt_ready = norm_all_to_xt(xn, (banks[0:2], banks[2:4]))
            for g in range(NG):
                dve.wait(got_bo)
                for b in range(GB):
                    bo_added = dve.do(V.tensor_tensor, X[:, g * GB + b, :], X[:, g * GB + b, :], bob, ALU.add)

            fill_banks = banks[0:2]
            nfill = [0]
            q_ready, k_ready, v_ready = {}, {}, {}
            qk_free = [None, None]
            v_free = [None, None]

            def fill(grp, i):
                hg, g = divmod(grp, NG)
                s, ws = grp % 2, hg % 2
                bank = fill_banks[nfill[0] % 2]
                nfill[0] += 1
                hi, lo = wr[ws]
                pe.wait(*weights_ready[hg], xt_ready[g])
                if i < 8:
                    m, h = divmod(i, HG)
                    cs, ts = slice(h * DH, (h + 1) * DH), slice(g * GT, (g + 1) * GT)
                    done = project(bank, [(hi[:, m, k, cs], lo[:, m, k, cs], XT[:, 0, k, ts], XT[:, 1, k, ts])
                                          for k in range(KT)])
                    act.wait(done, qk_free[s], got_bqs)
                    hh = hg * HG + h
                    if m == 0:
                        r = act.do(S.activation, qT[s][:, h, :], bank.t[:, :], ACT.Identity,
                                   bias=bqs[:, hh:hh + 1], scale=scale)
                        q_ready[grp] = r
                    else:
                        r = act.do(S.activation, kT[s][:, h, :], bank.t[:, :], ACT.Identity,
                                   bias=vec[:, H + hh:H + hh + 1])
                        k_ready[grp] = r
                else:
                    b = i - 8
                    ts = slice((g * GB + b) * P, (g * GB + b + 1) * P)
                    done = project(bank, [(XT[:, 0, k, ts], XT[:, 1, k, ts], hi[:, 2, k, :], lo[:, 2, k, :])
                                          for k in range(KT)])
                    dve.wait(done, v_free[s], got_bv)
                    r = dve.do(V.tensor_tensor, vv[s][:, b, :], bank.t[:, :],
                               bvb[:, hg * 512:(hg + 1) * 512], ALU.add)
                    v_ready[grp, b] = r
                bank.free = r
                wr_free[ws] = done

            sbank, tbank, zbank, obank = banks[2:4], banks[4:6], banks[6], banks[7]
            max_ready, exp_ready, probs_ready, pt_ready, z_ready = {}, {}, {}, {}, {}
            Sm_free, P_free, PT_free, ZT_free = [None] * 2, [None] * 2, [None] * 2, [None] * 2

            def scores(n):
                grp, b = divmod(n, GB)
                s, u = grp % 2, n % 2
                bank = sbank[u]
                pe.wait(bank.free, q_ready[grp], k_ready[grp])
                ts = slice(b * P, (b + 1) * P)
                for h in range(HG):
                    m = pe.do(T.matmul, bank.t[:, h * P:(h + 1) * P], qT[s][:, h, ts], kT[s][:, h, ts],
                              start=True, stop=True)
                qk_free[s] = m
                dve.wait(m, Sm_free[u], got_causal)
                m = bank.free = dve.do(V.tensor_tensor, Smask[u], four(bank.t[:, :]),
                                       causal.unsqueeze(1).broadcast_to([P, HG, P]), ALU.add)
                max_ready[n] = row_max(negmax[u], Smask[u], m)

            def exps(n):
                u = n % 2
                exp_ready[n] = Sm_free[u] = exponentials(Pm[u], Smask[u], negmax[u], sums[u], max_ready[n],
                                                         P_free[u])

            def norm(n):
                u = n % 2
                probs_ready[n] = normalise(Pm[u], sums[u], rinv[u], exp_ready[n])

            def transposes(n):
                u = n % 2
                bank = tbank[u]
                pe.wait(bank.free, probs_ready[n])
                for h in range(HG):
                    m = pe.do(T.transpose, bank.t[:, h * P:(h + 1) * P], Pm[u][:, h, :], ident[:, :])
                P_free[u] = m
                act.wait(m, PT_free[u])
                pt_ready[n] = bank.free = act.do(S.copy, PT[u], four(bank.t[:, :]))

            def values(n):
                grp, b = divmod(n, GB)
                s, u = grp % 2, n % 2
                pe.wait(zbank.free, pt_ready[n], v_ready[grp, b])
                for h in range(HG):
                    m = pe.do(T.matmul, zbank.t[:, h * P:(h + 1) * P], vv[s][:, b, h * DH:(h + 1) * DH],
                              PT[u][:, h, :], start=True, stop=True)
                PT_free[u] = m
                v_free[s] = m
                dve.wait(m, ZT_free[u])
                z_ready[n] = zbank.free = dve.do(V.tensor_copy, ZT[u], four(zbank.t[:, :]))

            def output(n):
                grp, b = divmod(n, GB)
                hg, g = divmod(grp, NG)
                u = n % 2
                pe.wait(obank.free, z_ready[n], wo_ready[hg])
                for h in range(HG):
                    m = pe.do(T.matmul, obank.t[:, 0:D], ZT[u][:, h, :], wo[hg % 2][:, h, :],
                              start=h == 0, stop=h == HG - 1)
                ZT_free[u] = m
                wo_free[hg % 2] = m
                dve.wait(m, bo_added if hg == 0 else x_ready[g])
                x_ready[g] = obank.free = dve.do(V.tensor_tensor, X[:, g * GB + b, :], obank.t[:, 0:D],
                                                 X[:, g * GB + b, :], ALU.add)

            for i in range(12):
                fill(0, i)
            fetch_weights(1)
            nsteps = NHG * NG * GB
            for n in range(nsteps + 1):
                grp, b = divmod(n, GB)
                nxt = grp + 1
                more = nxt < NHG * NG and n < nsteps
                if n < nsteps:
                    scores(n)
                if n >= 1:
                    transposes(n - 1)
                if n < nsteps:
                    exps(n)
                if more:
                    fill(nxt, 3 * b)
                if n >= 1:
                    values(n - 1)
                if more:
                    fill(nxt, 3 * b + 1)
                if n < nsteps:
                    norm(n)
                if n >= 1:
                    output(n - 1)
                if more:
                    fill(nxt, 3 * b + 2)
                if b == 0 and grp % NG == 0 and 0 < grp // NG < NHG - 1:
                    fetch_weights(grp // NG + 1)
            phase_end()

        def phase2(scope):
            ar, = phase_memory("wkv", scope, 0)
            xn = [ar.take(GB * D).rearrange("p (b d) -> p b d", b=GB) for _ in range(2)]
            ctxT = ar.take(KT * NT).rearrange("p (k t) -> p k t", k=KT)
            CH = GB * SEG

            def segs(slots):
                return [ar.take(CH).rearrange("p (b t) -> p b t", b=GB) for _ in range(slots)]
            key, peak, num, den = segs(2), segs(2), segs(2), segs(2)
            e2v, e2b = segs(2), segs(2)
            decay = segs(KT)
            e1b = segs(2)

            def flat(slots):
                return [ar.take(GT).rearrange("p (b t) -> p b t", b=GB) for _ in range(slots)]
            q, e1, e2, t1, t2, y = flat(2), flat(2), flat(2), flat(2), flat(2), flat(2)
            sm.at = small_base
            w = sm.take(KT)
            u_first = vec[:, 34:36]
            got_ctx = load("load_ctx2", ctxT, io["ctxT"])

            act.wait(got_vec)
            m = act.do(S.activation, w, vec[:, 32:34], ACT.Exp)
            dve.wait(m)
            m = dve.do(V.tensor_scalar, w, w, -1.0, None, ALU.mult)
            dve.wait(m)
            w_ready = m
            for kt in range(KT):
                m = dve.do(V.memset, decay[kt], 0.0)
                dve.wait(m)
                m = dve.do(V.tensor_scalar, decay[kt], decay[kt], w[:, kt:kt + 1], None, ALU.add)
                dve.wait(m)
                m = dve.do(V.memset, decay[kt][:, :, 0:1], -1e38)
            for s in range(2):
                dve.do(V.memset, key[s][:, :, 0:1], -1e38)
                dve.do(V.memset, e1b[s][:, :, 0:1], 0.0)
                dve.do(V.memset, e2v[s][:, :, 0:1], 0.0)
                m = dve.do(V.memset, e2b[s][:, :, 0:1], 0.0)
            dve.wait(m)
            init = m

            now, was = slice(1, SEG), slice(0, P)
            last_read = {}
            ybank = [banks[4], banks[5]]

            def chunk(g, kt, bank, done, c):
                s = c % 2
                lr = last_read.get(s)
                act.wait(done, init, lr)
                m = act.do(S.copy, key[s][:, :, now], bank.t[:, :].rearrange("p (b t) -> p b t", b=GB))
                bank.free = m
                k, v = key[s][:, :, now], ctxT[:, kt, g * GT:(g + 1) * GT].rearrange("p (b t) -> p b t", b=GB)
                dve.wait(m)
                m = dve.do(V.tensor_tensor_scan, peak[s].rearrange("p b t -> p (b t)"),
                           decay[kt].rearrange("p b t -> p (b t)"), key[s].rearrange("p b t -> p (b t)"),
                           -1e38, ALU.add, ALU.max)
                dve.wait(m)
                pool.wait(m)
                m3 = dve.do(V.scalar_tensor_tensor, out=e1b[s][:, :, now], in0=peak[s][:, :, was],
                            scalar=w[:, kt:kt + 1], in1=peak[s][:, :, now], op0=ALU.add, op1=ALU.subtract)
                m4 = pool.do(G.tensor_tensor, e2b[s][:, :, now], k, peak[s][:, :, now], ALU.subtract)
                m = dve.do(V.scalar_tensor_tensor, out=q[s], in0=k, scalar=u_first[:, kt:kt + 1],
                           in1=peak[s][:, :, was], op0=ALU.add, op1=ALU.max)
                act.wait(m3)
                m3 = act.do(S.activation, e1b[s][:, :, now], e1b[s][:, :, now], ACT.Exp)
                act.wait(m4)
                m4 = act.do(S.activation, e2b[s][:, :, now], e2b[s][:, :, now], ACT.Exp)
                dve.wait(m)
                m1 = dve.do(V.tensor_tensor, e1[s], peak[s][:, :, was], q[s], ALU.subtract)
                m2 = dve.do(V.scalar_tensor_tensor, out=e2[s], in0=k, scalar=u_first[:, kt:kt + 1],
                            in1=q[s], op0=ALU.add, op1=ALU.subtract)
                act.wait(m1)
                m1 = act.do(S.activation, e1[s], e1[s], ACT.Exp)
                act.wait(m2)
                m2 = act.do(S.activation, e2[s], e2[s], ACT.Exp)
                pool.wait(m4, got_ctx)
                mv_ = pool.do(G.tensor_tensor, e2v[s][:, :, now], e2b[s][:, :, now], v, ALU.mult)
                dve.wait(m3, m4)
                mb = dve.do(V.tensor_tensor_scan, den[s].rearrange("p b t -> p (b t)"),
                            e1b[s].rearrange("p b t -> p (b t)"), e2b[s].rearrange("p b t -> p (b t)"),
                            0.0, ALU.mult, ALU.add)
                dve.wait(mv_)
                ma = dve.do(V.tensor_tensor_scan, num[s].rearrange("p b t -> p (b t)"),
                            e1b[s].rearrange("p b t -> p (b t)"), e2v[s].rearrange("p b t -> p (b t)"),
                            0.0, ALU.mult, ALU.add)
                pool.wait(m2)
                pv = pool.do(G.tensor_tensor, t2[s], e2[s], v, ALU.mult)
                dve.wait(mb, m1)
                m = dve.do(V.tensor_tensor, t1[s], e1[s], den[s][:, :, was], ALU.mult)
                pool.wait(ma, m1)
                pa = pool.do(G.tensor_tensor, q[s], e1[s], num[s][:, :, was], ALU.mult)
                dve.wait(m, m2)
                m = dve.do(V.tensor_tensor, t1[s], t1[s], e2[s], ALU.add)
                dve.wait(m)
                m = dve.do(V.reciprocal, t1[s], t1[s])
                dve.wait(pa, pv)
                m2_ = dve.do(V.tensor_tensor, t2[s], t2[s], q[s], ALU.add)
                dve.wait(m, m2_)
                m = dve.do(V.tensor_tensor, y[s], t1[s], t2[s], ALU.mult)
                yb = ybank[s]
                pe.wait(m, yb.free)
                for b in range(GB):
                    m = pe.do(T.transpose, yb.t[:, b * P:(b + 1) * P], y[s][:, b, :], ident[:, :])
                return m

            def add_back(g, kt, s, m):
                dve.wait(m)
                last_read[s] = m
                ybank[s].free = x_ready[g] = dve.do(
                    V.tensor_tensor, X[:, g * GB:(g + 1) * GB, kt * P:(kt + 1) * P],
                    ybank[s].t[:, :].rearrange("p (b t) -> p b t", b=GB),
                    X[:, g * GB:(g + 1) * GB, kt * P:(kt + 1) * P], ALU.add)

            c = 0
            for g in range(NG):
                two = banks[2 * (g % 2):2 * (g % 2) + 2]
                moments(g)
                marks = normalised(g, xn)
                done = [to_channels(g, xn, marks, kt, two[kt]) for kt in range(KT)]
                for kt in range(KT):
                    m = chunk(g, kt, two[kt], done[kt], c)
                    add_back(g, kt, c % 2, m)
                    c += 1
            phase_end()

        def phase3(scope):
            wr, ar = phase_memory("experts", scope, 7168)
            raw = ar.take(NJ * JW).rearrange("p (j c) -> p j c", j=NJ)
            sel = ar.take(NJ * P // 2).bitcast(BF16)
            combT = ar.take(NT // 2).bitcast(BF16)
            gate = [ar.take(GT) for _ in range(2)]
            hid = [ar.take(GT) for _ in range(2)]
            sm.at = small_base
            wslot = [[wr.take(JW) for _ in range(2)] for _ in range(3)]
            hsplit = [[wr.take(GT) for _ in range(2)] for _ in range(2)]
            router = [wr.take(KT * P).rearrange("p (k c) -> p k c", k=KT) for _ in range(2)]
            tail = raw.rearrange("p j c -> p (j c)")[:, (NJ - 4) * JW:]
            xn = [tail[:, i * GB * D:(i + 1) * GB * D].rearrange("p (b d) -> p b d", b=GB) for i in range(2)]
            rraw = tail[:, 2 * GB * D:2 * GB * D + KT * P].rearrange("p (k c) -> p k c", k=KT)
            sp_first = NJ - 4
            got_router = load("load_router", rraw, io["router"])
            got_sel = load("load_sel", sel, io["sel"])
            got_w = {}
            per = 4
            for j in range(0, sp_first, per):
                m = load(f"load_moe{j}", raw[:, j:j + per, :], io["moe"][:, j:j + per, :])
                for i in range(j, j + per):
                    got_w[i] = m
            router_ready = split(router[0], router[1], rraw, [got_router], act, S.copy, dve, V.tensor_tensor)

            lt = hid[0]
            L = sm.take(GB * CW).rearrange("p (b c) -> p b c", b=GB)
            nm, zs, rz, s4, r4, sg = (sm.take(GB) for _ in range(6))
            PR = sm.take(GB * (TOPK + E)).rearrange("p (b c) -> p b c", b=GB)
            MR = sm.take(GB * (TOPK + E)).rearrange("p (b c) -> p b c", b=GB)
            top = sm.take(GB * 8).rearrange("p (b c) -> p b c", b=GB)
            C = sm.take(GB * CW).rearrange("p (b c) -> p b c", b=GB)
            CS = sm.take(GB * 64 // 2).bitcast(BF16).rearrange("p (b c) -> p b c", b=GB)
            rest = sm.take(GB * CW).rearrange("p (b c) -> p b c", b=GB)
            m = dve.do(V.memset, PR[:, :, 0:TOPK], 2.0)
            dve.do(V.memset, combT[:, :], 0.0)
            comb_zero = dve.mark

            comb_ready = []
            xt_ready = []
            rt_free = None
            for g in range(NG):
                moments(g)
                xt_ready.append(norm_to_xt(g, xn, banks[0:2]))
                pe.wait(xt_ready[g], router_ready)
                ts = slice(g * GT, (g + 1) * GT)
                done = project(banks[2], [(router[0][:, k, :], router[1][:, k, :], XT[:, 0, k, ts], XT[:, 1, k, ts])
                                          for k in range(KT)])
                act.wait(done, rt_free)
                m = banks[2].free = act.do(S.copy, lt[0:32, :], banks[2].t[0:32, :])
                pe.wait(m, banks[3].free)
                for b in range(GB):
                    m = pe.do(T.transpose, banks[3].t[:, b * 32:(b + 1) * 32], lt[0:32, b * P:(b + 1) * P],
                              ident[0:32, 0:32])
                rt_free = m
                dve.wait(m)
                bt = banks[3].t[:, 0:GB * 32].rearrange("p (b c) -> p b c", b=GB)
                m = banks[3].free = dve.do(V.tensor_copy, L, bt[:, :, 0:CW])
                dve.wait(m)
                m = dve.do(V.tensor_reduce, nm, L[:, :, 0:E], AX.X, ALU.max)
                dve.wait(m)
                m = dve.do(V.tensor_tensor, L[:, :, 0:E], L[:, :, 0:E], nm.unsqueeze(2).broadcast_to([P, GB, E]),
                           ALU.subtract)
                act.wait(m)
                m = act.do(S.activation, L[:, :, 0:E], L[:, :, 0:E], ACT.Exp)
                msg = act.do(S.activation, sg, L[:, :, E], ACT.Exp, scale=-1.0)
                dve.wait(m)
                m = dve.do(V.tensor_reduce, zs, L[:, :, 0:E], AX.X, ALU.add)
                dve.wait(m)
                m = dve.do(V.reciprocal, rz, zs)
                dve.wait(m, msg)
                m = dve.do(V.tensor_tensor, PR[:, :, TOPK:], L[:, :, 0:E], rz.unsqueeze(2).broadcast_to([P, GB, E]),
                           ALU.mult)
                msg = dve.do(V.tensor_scalar, sg, sg, 1.0, None, ALU.add)
                dve.wait(m, msg)
                for b in range(GB):
                    m = dve.do(V.max, top[:, b, :], PR[:, b, :])
                dve.wait(m)
                for b in range(GB):
                    m = dve.do(V.match_replace, MR[:, b, :], top[:, b, :], PR[:, b, :], 0.0)
                dve.wait(m)
                m = dve.do(V.tensor_tensor, rest[:, :, 0:E], PR[:, :, TOPK:], MR[:, :, TOPK:], ALU.subtract)
                msg = dve.do(V.reciprocal, C[:, :, E], sg)
                dve.wait(m)
                m = dve.do(V.tensor_reduce, s4, rest[:, :, 0:E], AX.X, ALU.add)
                dve.wait(m)
                m = dve.do(V.tensor_scalar, s4, s4, 1e-9, None, ALU.max)
                dve.wait(m)
                m = dve.do(V.reciprocal, r4, s4)
                dve.wait(m)
                m = dve.do(V.tensor_tensor, C[:, :, 0:E], rest[:, :, 0:E],
                           r4.unsqueeze(2).broadcast_to([P, GB, E]), ALU.mult)
                dve.wait(m, msg)
                src = C
                for part in range(NSPLIT):
                    piece = CS[:, :, part * CW:(part + 1) * CW]
                    m = dve.do(V.tensor_copy, piece, src)
                    dve.wait(m)
                    if part < NSPLIT - 1:
                        m = dve.do(V.tensor_tensor, rest, src, piece, ALU.subtract)
                        dve.wait(m)
                        src = rest
                pe.wait(m, got_idb, banks[4].free)
                bb = banks[4].t[:, :].bitcast(BF16)
                for b in range(GB):
                    m = pe.do(T.transpose, bb[0:NSPLIT * CW, b * P:(b + 1) * P], CS[:, b, 0:NSPLIT * CW],
                              identb[:, :])
                dve.wait(m)
                banks[4].free = m = dve.do(V.tensor_copy, combT[0:NSPLIT * CW, ts], bb[0:NSPLIT * CW, 0:GT])
                comb_ready.append(m)
            sp.wait(pe.mark, dve.mark, act.mark)
            m = load("load_moe_tail", raw[:, sp_first:, :], io["moe"][:, sp_first:, :])
            for i in range(sp_first, NJ):
                got_w[i] = m

            acc = banks[0:2]
            ring = banks[2:8]
            nring = [0]

            def next_bank():
                nring[0] += 1
                return ring[(nring[0] - 1) % 6]

            w_free = [None] * 3
            w_ready = {}
            h_ready = {}
            hs_free = [None] * 2
            gate_free, hid_free = [None] * 2, [None] * 2
            steps = [(g, j) for g in range(NG) for j in range(NJ)]

            def split_weights(n):
                g, j = steps[n]
                s = n % 3
                w_ready[n] = split(wslot[s][0], wslot[s][1], raw[:, j, :], [got_w[j], w_free[s]],
                                   dve, V.tensor_copy, pool, G.tensor_tensor)

            def up(n):
                g, j = steps[n]
                s, u = n % 3, n % 2
                hi, lo = (wslot[s][i].rearrange("p (m c) -> p m c", m=6) for i in range(2))
                ts = slice(g * GT, (g + 1) * GT)
                pe.wait(w_ready[n], comb_ready[g])
                got = []
                for m in range(2):
                    bank = next_bank()
                    done = project(bank, [(hi[:, 2 * m + k, :], lo[:, 2 * m + k, :], XT[:, 0, k, ts], XT[:, 1, k, ts])
                                          for k in range(KT)])
                    got.append((bank, done))
                bank = next_bank()
                pe.wait(bank.free, got_sel)
                done = pe.do(T.matmul, bank.t[:, :], sel[:, j * P:(j + 1) * P], combT[:, ts], start=True, stop=True)
                (gb, gd), (ub, ud), (cb, cd) = got[0], got[1], (bank, done)
                act.wait(gd, gate_free[u])
                gb.free = m = act.do(S.activation, gate[u], gb.t[:, :], ACT.Silu)
                dve.wait(m, ud, hid_free[u])
                gate_free[u] = ub.free = m = dve.do(V.tensor_tensor, hid[u], gate[u], ub.t[:, :], ALU.mult)
                dve.wait(m, cd)
                cb.free = m = dve.do(V.tensor_tensor, hid[u], hid[u], cb.t[:, :], ALU.mult)
                h_ready[n] = hid_free[u] = split(hsplit[u][0], hsplit[u][1], hid[u], [m, hs_free[u]],
                                                 act, S.copy, pool, G.tensor_tensor)

            def down(n):
                g, j = steps[n]
                s, u = n % 3, n % 2
                hi, lo = wslot[s]
                pe.wait(h_ready[n])
                for d in range(KT):
                    if j == 0:
                        pe.wait(acc[d].free)
                    cs = slice(4 * P + d * P, 4 * P + (d + 1) * P)
                    first, last = j == 0, j == NJ - 1
                    pe.quiet(T.matmul, acc[d].t[:, :], hi[:, cs], hsplit[u][0], start=first, stop=False)
                    pe.quiet(T.matmul, acc[d].t[:, :], hi[:, cs], hsplit[u][1], start=False, stop=False)
                    m = pe.do(T.matmul, acc[d].t[:, :], lo[:, cs], hsplit[u][0], start=False, stop=last)
                w_free[s] = hs_free[u] = m
                if last:
                    for d in range(KT):
                        act.wait(m, gate_free[d], hid_free[d])
                        acc[d].free = r = act.do(S.copy, gate[d], acc[d].t[:, :])
                        bank = next_bank()
                        pe.wait(r, bank.free)
                        for b in range(GB):
                            r = pe.do(T.transpose, bank.t[:, b * P:(b + 1) * P], gate[d][:, b * P:(b + 1) * P],
                                      ident[:, :])
                        gate_free[d] = r
                        dve.wait(r)
                        bank.free = x_ready[g] = dve.do(
                            V.tensor_tensor, X[:, g * GB:(g + 1) * GB, d * P:(d + 1) * P],
                            bank.t[:, :].rearrange("p (b t) -> p b t", b=GB),
                            X[:, g * GB:(g + 1) * GB, d * P:(d + 1) * P], ALU.add)

            n = len(steps)
            split_weights(0)
            split_weights(1)
            for i in range(n + 1):
                if i < n:
                    up(i)
                if i >= 1:
                    down(i - 1)
                if i + 2 < n:
                    split_weights(i + 2)
            phase_end()


        def phase4(scope):
            wr, ar = phase_memory("narrow_attention", scope, 2 * KT * 3 * D)
            w_hi, w_lo = (wr.take(KT * 3 * D).rearrange("p (k c) -> p k c", k=KT) for _ in range(2))
            raw = ar.take(KT * 3 * D).rearrange("p (k c) -> p k c", k=KT)
            wo = ar.take(KT * D).rearrange("p (k c) -> p k c", k=KT)
            bias, bo = ar.take(3 * D), ar.take(D)
            mask8 = ar.take(8)
            xn = [ar.take(GB * D).rearrange("p (b d) -> p b d", b=GB) for _ in range(2)]
            qk = [ar.take(2 * D) for _ in range(GB)]
            vv = [ar.take(D) for _ in range(2 * GB)]
            qsq = ar.take(2 * D)
            qT = [ar.take(2 * P).rearrange("p (i t) -> p i t", i=2) for _ in range(2 * GB)]
            kT = [ar.take(2 * P).rearrange("p (i t) -> p i t", i=2) for _ in range(2 * GB)]
            kbd = [ar.take(2 * 8 * P).rearrange("p (i h t) -> p i h t", i=2, h=8) for _ in range(2)]
            Pm = [ar.take(512).rearrange("p (h k) -> p h k", h=HG) for _ in range(2)]
            PT = [ar.take(512).rearrange("p (h k) -> p h k", h=HG) for _ in range(2)]
            z = [ar.take(D) for _ in range(2)]
            zT = [ar.take(2 * P).rearrange("p (i t) -> p i t", i=2) for _ in range(2)]
            sm.at = small_base
            qss = sm.take(2 * GB * 32).rearrange("p (s b c) -> p s b c", s=2, b=GB)
            gg = sm.take(2)
            negmax = [sm.take(HG) for _ in range(2)]
            rowsum = [sm.take(H) for _ in range(2)]
            rinv = [sm.take(H) for _ in range(2)]

            got_w = load("load_w4", raw, io["wqkv1"])
            got_wo = load("load_wo4", wo, io["wo1"])
            got_bias = load("load_bias4", bias, io["bqkv1"].partition_broadcast(P))
            got_bo = load("load_bo4", bo, io["bo1"].partition_broadcast(P))
            got_mask8 = load("load_mask8", mask8, io["mask8"])
            dve.wait(got_w, got_vec)
            for k in range(KT):
                dve.do(V.tensor_scalar, raw[:, k, 0:D], raw[:, k, 0:D], vec[:, 36 + k:37 + k], None, ALU.mult)
                m = dve.do(V.tensor_scalar, raw[:, k, D:], raw[:, k, D:], vec[:, 38 + k:39 + k], None, ALU.mult)
            w_ready = split(w_hi, w_lo, raw, [m], act, S.copy, pool, G.tensor_tensor)
            m = dve.do(V.tensor_tensor, gg[:, 0:1], vec[:, 40:41], vec[:, 40:41], ALU.mult)
            dve.wait(m)
            gg_ready = dve.do(V.tensor_scalar, gg[:, 0:1], gg[:, 0:1], float(DS) ** -0.5, None, ALU.mult)

            fb, sbank, tbank, zbank, obank = banks[0:2], banks[2:4], banks[4:6], banks[6], banks[7]
            xt_ready, bo_added = {}, {}
            qk_ready, v_ready, head_ready, kt_ready, kbd_ready = {}, {}, {}, {}, {}
            v_free, kt_free, qt_free = [None] * 8, [None] * 8, [None] * 8
            head_normed = {}
            qk_free, kbd_free = [None] * GB, [None] * 2
            qsq_free = [None]

            tiles = {}

            def prep_moments(g):
                moments(g, then_rms=True)

            def prep_norm(g):
                tiles[g] = normalised(g, xn)

            def prep_channels(g, kt):
                xt_ready[g] = split_channels(g, xn, tiles[g], kt, fb[kt])

            def prep_bias(g):
                dve.wait(got_bo, tiles[g][-1])
                for b in range(GB):
                    m = dve.do(V.tensor_tensor, X[:, g * GB + b, :], X[:, g * GB + b, :], bo, ALU.add)
                bo_added[g] = m

            def prep_project(g, b):
                bb = g * GB + b
                ts = slice(bb * P, (bb + 1) * P)
                pe.wait(xt_ready[g], w_ready)
                done = project(fb[0], [(XT[:, 0, k, ts], XT[:, 1, k, ts], w_hi[:, k, 0:512], w_lo[:, k, 0:512])
                                       for k in range(KT)])
                dve.wait(done, got_bias, qk_free[b])
                m = fb[0].free = dve.do(V.tensor_tensor, qk[b], fb[0].t[:, :], bias[:, 0:512], ALU.add)
                done = project(fb[1], [(XT[:, 0, k, ts], XT[:, 1, k, ts], w_hi[:, k, 512:], w_lo[:, k, 512:])
                                       for k in range(KT)])
                dve.wait(done, v_free[bb % 8])
                v_ready[bb] = fb[1].free = dve.do(V.tensor_tensor, vv[bb % 8], fb[1].t[:, 0:D], bias[:, 512:],
                                                  ALU.add)
                pool.wait(m, qsq_free[0])
                m = pool.do(G.tensor_tensor, qsq, qk[b], qk[b], ALU.mult)
                dve.wait(m)
                qsq_free[0] = qk_ready[bb] = dve.do(V.tensor_reduce, qss[:, g % 2, b, :],
                                                    qsq.rearrange("p (c d) -> p c d", d=DS), AX.X, ALU.add)

            def prep_scale(g):
                s = g % 2
                act.wait(qk_ready[g * GB + GB - 1])
                head_ready[g] = act.do(S.activation, qss[:, s], qss[:, s], ACT.Sqrt, bias=eps_rms[:, 0:1],
                                       scale=1.0 / DS)

            def prep_head_norm(g):
                s = g % 2
                dve.wait(head_ready[g])
                pool.wait(dve.do(V.reciprocal, qss[:, s], qss[:, s]))
                for b in range(GB):
                    r3 = qk[b].rearrange("p (c d) -> p c d", d=DS)
                    head_normed[g * GB + b] = pool.do(
                        G.tensor_tensor, r3, r3, qss[:, s, b, :].unsqueeze(2).broadcast_to([P, 32, DS]), ALU.mult)

            def prep_heads(g, b):
                bb = g * GB + b
                pe.wait(head_normed[bb], fb[0].free)
                for i in range(4):
                    m = pe.do(T.transpose, fb[0].t[:, i * P:(i + 1) * P], qk[b][:, i * P:(i + 1) * P], ident[:, :])
                qk_free[b] = m
                act.wait(m, qt_free[bb % 8], kt_free[bb % 8], gg_ready)
                act.do(S.activation, qT[bb % 8], fb[0].t[:, 0:256].rearrange("p (i t) -> p i t", i=2),
                       ACT.Identity, scale=gg[:, 0:1])
                kt_ready[bb] = fb[0].free = act.do(S.copy, kT[bb % 8],
                                                   fb[0].t[:, 256:512].rearrange("p (i t) -> p i t", i=2))

            def spread_keys(bb):
                s = bb % 2
                pool.wait(kt_ready[bb], kbd_free[s], got_mask8)
                for i in range(2):
                    m = pool.do(G.tensor_tensor, kbd[s][:, i], kT[bb % 8][:, i].unsqueeze(1).broadcast_to([P, 8, P]),
                                mask8.unsqueeze(2).broadcast_to([P, 8, P]), ALU.mult)
                kt_free[bb % 8] = kbd_ready[bb] = m

            probs_ready, exp_ready, pt_ready = {}, {}, {}
            P_free, PT_free, z_free, zT_free = [None] * 2, [None] * 2, [None] * 2, [None] * 2

            def scores(n):
                bb, q4 = divmod(n, 4)
                u, s = n % 2, bb % 2
                bank = sbank[u]
                pe.wait(bank.free, kbd_ready[bb])
                m = pe.do(T.matmul, bank.t[:, :], qT[bb % 8][:, q4 // 2, :],
                          kbd[s][:, q4 // 2, (q4 % 2) * 4:(q4 % 2) * 4 + 4, :].rearrange("p h t -> p (h t)"),
                          start=True, stop=True)
                kbd_free[s] = qt_free[bb % 8] = m
                s4 = bank.t[:, :].rearrange("p (h k) -> p h k", h=HG)
                dve.wait(m)
                m = dve.do(V.tensor_reduce, negmax[u], s4, AX.X, ALU.max, negate=True)
                act.wait(m, P_free[u])
                for h in range(HG):
                    m = act.do(S.activation, Pm[u][:, h, :], s4[:, h, :], ACT.Exp, bias=negmax[u][:, h:h + 1],
                               accum_out=rowsum[s][:, q4 * 4 + h:q4 * 4 + h + 1])
                bank.free = exp_ready[n] = m

            def transposes(n):
                u = n % 2
                bank = tbank[u]
                pe.wait(bank.free, exp_ready[n])
                for h in range(HG):
                    m = pe.do(T.transpose, bank.t[:, h * P:(h + 1) * P], Pm[u][:, h, :], ident[:, :])
                P_free[u] = m
                dve.wait(m, PT_free[u])
                pt_ready[n] = bank.free = dve.do(V.tensor_copy, PT[u], bank.t[:, :].rearrange(
                    "p (h k) -> p h k", h=HG))

            def values(n):
                bb, q4 = divmod(n, 4)
                u, s = n % 2, bb % 2
                pe.wait(pt_ready[n], v_ready[bb])
                if q4 == 0:
                    pe.wait(zbank.free)
                for h in range(HG):
                    hh = q4 * HG + h
                    m = pe.do(T.matmul, zbank.t[:, hh * DS:(hh + 1) * DS], PT[u][:, h, :],
                              vv[bb % 8][:, hh * DS:(hh + 1) * DS], start=True, stop=True)
                PT_free[u] = m
                if q4 == 3:
                    v_free[bb % 8] = m
                    dve.wait(exp_ready[n])
                    r = dve.do(V.reciprocal, rinv[s], rowsum[s])
                    dve.wait(m, r, z_free[s])
                    z_done[bb] = zbank.free = dve.do(
                        V.tensor_tensor, z[s].rearrange("p (h d) -> p h d", h=H),
                        zbank.t[:, 0:D].rearrange("p (h d) -> p h d", h=H),
                        rinv[s].unsqueeze(2).broadcast_to([P, H, DS]), ALU.mult)

            z_done = {}

            def output(bb):
                s, g = bb % 2, bb // GB
                pe.wait(z_done[bb], obank.free)
                for i in range(2):
                    m = pe.do(T.transpose, obank.t[:, i * P:(i + 1) * P], z[s][:, i * P:(i + 1) * P], ident[:, :])
                z_free[s] = m
                act.wait(m, zT_free[s])
                m = act.do(S.copy, zT[s], obank.t[:, 0:256].rearrange("p (i t) -> p i t", i=2))
                pe.wait(m, got_wo)
                for i in range(2):
                    m = pe.do(T.matmul, obank.t[:, 256:512], zT[s][:, i, :], wo[:, i, :], start=i == 0, stop=i == 1)
                zT_free[s] = m
                dve.wait(m, bo_added[g], x_ready[g])
                x_ready[g] = obank.free = dve.do(V.tensor_tensor, X[:, bb, :], obank.t[:, 256:512], X[:, bb, :],
                                                 ALU.add)

            def preparation(g):
                return {0: [(prep_moments, g)], 1: [(prep_norm, g)], 2: [(prep_channels, g, 0), (prep_channels, g, 1)],
                        3: [(prep_project, g, 0)], 4: [(prep_project, g, 1)], 5: [(prep_project, g, 2)],
                        6: [(prep_project, g, 3)], 7: [(prep_scale, g), (prep_bias, g)], 8: [(prep_head_norm, g)],
                        10: [(prep_heads, g, 0)], 11: [(prep_heads, g, 1)], 12: [(prep_heads, g, 2)],
                        13: [(prep_heads, g, 3)]}

            for at, work in sorted(preparation(0).items()):
                for fn, *args in work:
                    fn(*args)
            spread_keys(0)
            steps = B * 4
            for n in range(steps + 4):
                g, u = divmod(n, 16)
                if n < steps:
                    if n % 4 == 0 and n // 4 + 1 < B:
                        spread_keys(n // 4 + 1)
                    scores(n)
                if g + 1 < NG and n < steps:
                    for fn, *args in preparation(g + 1).get(u, []):
                        fn(*args)
                if 1 <= n <= steps:
                    transposes(n - 1)
                if 2 <= n <= steps + 1:
                    values(n - 2)
                if n >= 7 and (n - 7) % 4 == 0:
                    output((n - 7) // 4)
            phase_end()

        def phase5(scope):
            wr, ar = phase_memory("cross_attention", scope, 8192)
            kv_hi, kv_lo = (wr.take(KT * 2 * 512).rearrange("p (k c) -> p k c", k=KT) for _ in range(2))
            wq = [[wr.take(KT * 512).rearrange("p (k c) -> p k c", k=KT) for _ in range(2)] for _ in range(2)]
            kT = ar.take(B * NKV * P).rearrange("p (b h t) -> p b h t", b=B, h=NKV)
            vv = ar.take(B * NKV * DH).rearrange("p (b c) -> p b c", b=B)
            shared = ar.at
            sm.at = small_base
            kscale = sm.take(2)
            kss = sm.take(2 * GB * NKV).rearrange("p (s b c) -> p s b c", s=2, b=GB)
            small_here = sm.at

            raw = ar.take(KT * 2 * 512).rearrange("p (k c) -> p k c", k=KT)
            bias = ar.take(2 * 512)
            stage = [ar.take(KT * GT).rearrange("p (k t) -> p k t", k=KT) for _ in range(2)]
            key = [ar.take(512) for _ in range(2 * GB)]
            ksq = ar.take(512)
            got_w = load("load_wkv5", raw, io["wkvx"])
            got_bias = load("load_bias5", bias, io["bkvx"].partition_broadcast(P))
            w_ready = split(kv_hi, kv_lo, raw, [got_w], act, S.copy, pool, G.tensor_tensor)
            dve.wait(got_vec)
            m = dve.do(V.tensor_tensor, kscale[:, 0:1], vec[:, 57:58], vec[:, 58:59], ALU.mult)
            dve.wait(m)
            kscale_ready = dve.do(V.tensor_scalar, kscale[:, 0:1], kscale[:, 0:1],
                                  1.0 / float(np.sqrt(np.float32(DH))), None, ALU.mult)
            stage_free = [None] * 2
            ct_ready = []
            for g in range(NG):
                ts = slice(g * GT, (g + 1) * GT)
                sp.wait(stage_free[g % 2])
                got = load(f"load_ctx5_{g}", stage[g % 2], io["ctxT"][:, :, ts])
                stage_free[g % 2] = m = split(XT[:, 0, :, ts], XT[:, 1, :, ts], stage[g % 2], [got],
                                              act, S.copy, dve, V.tensor_tensor)
                ct_ready.append(m)
            key_free = [None] * 8
            ksq_free = None
            ring, at = banks[0:6], 0

            def heads_out(g):
                s = g % 2
                act.wait(ksq_free)
                m = act.do(S.activation, kss[:, s], kss[:, s], ACT.Sqrt, bias=eps_qk[:, 0:1], scale=1.0 / DH)
                dve.wait(m)
                r = dve.do(V.reciprocal, kss[:, s], kss[:, s])
                for b in range(GB):
                    kb = key[(g * GB + b) % 8]
                    k3 = kb.rearrange("p (h d) -> p h d", h=NKV)
                    pool.wait(r)
                    m = pool.do(G.tensor_tensor, k3, k3, kss[:, s, b, :].unsqueeze(2).broadcast_to([P, NKV, DH]),
                                ALU.mult)
                    bank = banks[6 + b % 2]
                    pe.wait(m, bank.free)
                    for h in range(NKV):
                        m = pe.do(T.transpose, bank.t[:, h * P:(h + 1) * P], kb[:, h * P:(h + 1) * P], ident[:, :])
                    key_free[(g * GB + b) % 8] = m
                    act.wait(m, kscale_ready)
                    bank.free = act.do(S.activation, kT[:, g * GB + b], bank.t[:, :].rearrange(
                        "p (h t) -> p h t", h=NKV), ACT.Identity, scale=kscale[:, 0:1])

            for g in range(NG):
                for b in range(GB):
                    bb = g * GB + b
                    ts = slice(bb * P, (bb + 1) * P)
                    pe.wait(ct_ready[g], w_ready)
                    kbank, vbank = ring[at % 6], ring[(at + 1) % 6]
                    at += 2
                    done = project(kbank, [(XT[:, 0, k, ts], XT[:, 1, k, ts], kv_hi[:, k, 0:512], kv_lo[:, k, 0:512])
                                           for k in range(KT)])
                    dve.wait(done, got_bias, key_free[bb % 8])
                    m = kbank.free = dve.do(V.tensor_tensor, key[bb % 8], kbank.t[:, :], bias[:, 0:512], ALU.add)
                    done = project(vbank, [(XT[:, 0, k, ts], XT[:, 1, k, ts], kv_hi[:, k, 512:], kv_lo[:, k, 512:])
                                           for k in range(KT)])
                    dve.wait(done)
                    vbank.free = dve.do(V.tensor_tensor, vv[:, bb, :], vbank.t[:, :], bias[:, 512:], ALU.add)
                    act.wait(m, ksq_free)
                    m = act.do(S.activation, ksq, key[bb % 8], ACT.Square)
                    dve.wait(m)
                    ksq_free = dve.do(V.tensor_reduce, kss[:, g % 2, b, :],
                                      ksq.rearrange("p (h d) -> p h d", h=NKV), AX.X, ALU.add)
                if g >= 1:
                    heads_out(g - 1)
            heads_out(NG - 1)
            phase_end()

            ar.at = shared
            raw = ar.take(KT * 512).rearrange("p (k c) -> p k c", k=KT)
            wo = [ar.take(HG * D).rearrange("p (h d) -> p h d", h=HG) for _ in range(2)]
            qT = [ar.take(HG * GT).rearrange("p (h t) -> p h t", h=HG) for _ in range(2)]
            qsq = [ar.take(GT) for _ in range(2)]
            Smask, Pm, PT, ZT = ([four(ar.take(512)) for _ in range(2)] for _ in range(4))
            mask = ar.take(P)
            xn = [ar.take(GB * D).rearrange("p (b d) -> p b d", b=GB) for _ in range(2)]
            sm.at = small_here
            negmax = [sm.take(HG) for _ in range(2)]
            sums = [sm.take(HG) for _ in range(2)]
            rinv = [sm.take(HG) for _ in range(2)]
            rq = [sm.take(GB * HG) for _ in range(2)]
            ones = sm.take(2)
            ones_ready = dve.do(V.memset, ones, 1.0)
            got_mask = load("load_mask5", mask, io["mask"])

            weights_ready, wo_ready = {}, {}
            raw_free, wr_free, wo_free = [None], [None] * 2, [None] * 2

            def fetch_weights(hg):
                s = hg % 2
                sp.wait(raw_free[0], wo_free[s])
                got = load(f"load_wq5_{hg}", raw, io["wqx"][:, hg])
                wo_ready[hg] = load(f"load_wo5_{hg}", wo[s], io["wox"][:, hg])
                hq, hop, lq, lop = (act, S.copy, dve, V.tensor_tensor) if hg == 0 else \
                                   (pool, G.tensor_copy, pool, G.tensor_tensor)
                raw_free[0] = weights_ready[hg] = split(wq[s][0], wq[s][1], raw, [got, wr_free[s]],
                                                        hq, hop, lq, lop)

            fetch_weights(0)
            xt_ready = norm_all_to_xt(xn, (banks[0:2], banks[2:4]))

            sbank, tbank, qbank, zbank, obank = banks[2:4], banks[4], banks[5], banks[6], banks[7]
            nfill = [0]
            q_ready, rq_ready = {}, {}
            q_free, q_squared, rq_free, qsq_free = [None] * 2, [None] * 2, [None] * 2, [None] * 2
            qsq_ready = {}

            def fill(grp, h):
                hg, g = divmod(grp, NG)
                s, hh = grp % 2, hg * HG + h
                bank = banks[nfill[0] % 2]
                nfill[0] += 1
                cs, ts = slice(h * DH, (h + 1) * DH), slice(g * GT, (g + 1) * GT)
                hi, lo = wq[hg % 2]
                pe.wait(weights_ready[hg], xt_ready[g])
                done = project(bank, [(hi[:, k, cs], lo[:, k, cs], XT[:, 0, k, ts], XT[:, 1, k, ts])
                                      for k in range(KT)])
                wr_free[hg % 2] = done
                act.wait(done, q_free[s], q_squared[s])
                m = bank.free = q_ready[grp] = act.do(S.activation, qT[s][:, h, :], bank.t[:, :], ACT.Identity,
                                                      bias=vec[:, 41 + hh:42 + hh])
                pool.wait(m, qsq_free[h % 2])
                q_squared[s] = qsq_ready[grp, h] = pool.do(G.tensor_tensor, qsq[h % 2], qT[s][:, h, :],
                                                           qT[s][:, h, :], ALU.mult)

            def sum_squares(grp, h):
                s = grp % 2
                pe.wait(qsq_ready[grp, h], qbank.free, ones_ready)
                for b in range(GB):
                    c = b * HG + h
                    m = pe.do(T.matmul, qbank.t[:, c:c + 1], qsq[h % 2][:, b * P:(b + 1) * P], ones[:, 0:1],
                              start=True, stop=True)
                qsq_free[h % 2] = m
                if h == HG - 1:
                    act.wait(m, rq_free[s])
                    m = qbank.free = act.do(S.activation, rq[s], qbank.t[:, 0:GB * HG], ACT.Sqrt,
                                            bias=eps_qk[:, 0:1], scale=1.0 / DH)
                    dve.wait(m)
                    rq_ready[grp] = dve.do(V.reciprocal, rq[s], rq[s])

            max_ready, exp_ready, probs_ready, pt_ready, z_ready = {}, {}, {}, {}, {}
            Sm_free, P_free, PT_free, ZT_free = [None] * 2, [None] * 2, [None] * 2, [None] * 2

            def scores(n):
                grp, b = divmod(n, GB)
                hg, g = divmod(grp, NG)
                s, u = grp % 2, n % 2
                bank = sbank[u]
                pe.wait(bank.free, q_ready[grp])
                ts = slice(b * P, (b + 1) * P)
                for h in range(HG):
                    m = pe.do(T.matmul, bank.t[:, h * P:(h + 1) * P], qT[s][:, h, ts], kT[:, g * GB + b, hg, :],
                              start=True, stop=True)
                q_free[s] = m
                dve.wait(m, Sm_free[u], rq_ready[grp], got_mask)
                for h in range(HG):
                    c = b * HG + h
                    m = dve.do(V.scalar_tensor_tensor, out=Smask[u][:, h, :], in0=bank.t[:, h * P:(h + 1) * P],
                               scalar=rq[s][:, c:c + 1], in1=mask, op0=ALU.mult, op1=ALU.add)
                bank.free = rq_free[s] = m
                max_ready[n] = row_max(negmax[u], Smask[u], m)

            def exps(n):
                u = n % 2
                exp_ready[n] = Sm_free[u] = exponentials(Pm[u], Smask[u], negmax[u], sums[u], max_ready[n],
                                                         P_free[u])

            def norm(n):
                u = n % 2
                probs_ready[n] = normalise(Pm[u], sums[u], rinv[u], exp_ready[n])

            def transposes(n):
                u, bank = n % 2, tbank
                pe.wait(bank.free, probs_ready[n])
                for h in range(HG):
                    m = pe.do(T.transpose, bank.t[:, h * P:(h + 1) * P], Pm[u][:, h, :], ident[:, :])
                P_free[u] = m
                act.wait(m, PT_free[u])
                pt_ready[n] = bank.free = act.do(S.copy, PT[u], four(bank.t[:, :]))

            def values(n):
                grp, b = divmod(n, GB)
                hg, g = divmod(grp, NG)
                u = n % 2
                pe.wait(zbank.free, pt_ready[n])
                m = pe.do(T.matmul, zbank.t[:, :], vv[:, g * GB + b, hg * DH:(hg + 1) * DH],
                          PT[u].rearrange("p h k -> p (h k)"), start=True, stop=True)
                PT_free[u] = m
                dve.wait(m, ZT_free[u])
                z_ready[n] = zbank.free = dve.do(V.tensor_copy, ZT[u], four(zbank.t[:, :]))

            def output(n):
                grp, b = divmod(n, GB)
                hg, g = divmod(grp, NG)
                u = n % 2
                pe.wait(obank.free, z_ready[n], wo_ready[hg])
                for h in range(HG):
                    m = pe.do(T.matmul, obank.t[:, 0:D], ZT[u][:, h, :], wo[hg % 2][:, h, :],
                              start=h == 0, stop=h == HG - 1)
                ZT_free[u] = m
                wo_free[hg % 2] = m
                dve.wait(m, x_ready[g])
                x_ready[g] = obank.free = dve.do(V.tensor_tensor, X[:, g * GB + b, :], obank.t[:, 0:D],
                                                 X[:, g * GB + b, :], ALU.add)

            for h in range(HG):
                fill(0, h)
                sum_squares(0, h)
            fetch_weights(1)
            fill(1, 0)
            to_sum = (1, 0)
            nsteps = NHG * NG * GB
            for n in range(nsteps + 1):
                grp, b = divmod(n, GB)
                ahead, h = divmod(n + GB + 1, GB)
                more = ahead < NHG * NG
                if n < nsteps:
                    scores(n)
                if n >= 1:
                    transposes(n - 1)
                if n < nsteps:
                    exps(n)
                if more:
                    fill(ahead, h)
                if n >= 1:
                    values(n - 1)
                if to_sum is not None:
                    sum_squares(*to_sum)
                to_sum = (ahead, h) if more else None
                if n < nsteps:
                    norm(n)
                if n >= 1:
                    output(n - 1)
                if b == 0 and grp % NG == 0 and 0 < grp // NG < NHG - 1:
                    fetch_weights(grp // NG + 1)
            phase_end()

        def phase6(scope):
            ar, = phase_memory("bitnet", scope, 0)
            raw = ar.take(2 * KT * BI + BJ * D)
            gu, dn = raw[:, 0:2 * KT * BI], raw[:, 2 * KT * BI:]
            tmp = ar.take(2 * KT * BI + BJ * D)
            wq = ar.take((2 * KT * BI + BJ * D) // 2).bitcast(BF16)
            wgu = wq[:, 0:2 * KT * BI].rearrange("p (m k c) -> p m k c", m=2, k=KT)
            wdn = wq[:, 2 * KT * BI:].rearrange("p (j d) -> p j d", j=BJ)
            xn = [ar.take(GB * D).rearrange("p (b d) -> p b d", b=GB) for _ in range(2)]
            xr = [ar.take(GB * D) for _ in range(2)]
            xq = [ar.take(GB * D // 2).bitcast(BF16) for _ in range(2)]
            xqT = [ar.take(GB * D // 2).bitcast(BF16).rearrange("p (k t) -> p k t", k=KT) for _ in range(2)]
            sg = [ar.take(BI) for _ in range(2)]
            hid = [ar.take(BI) for _ in range(2)]
            hq = [ar.take(BJ * P // 2).bitcast(BF16) for _ in range(2)]
            hT = [ar.take(BJ * P // 2).bitcast(BF16).rearrange("p (j t) -> p j t", j=BJ) for _ in range(2)]
            ones = ar.take(P)
            sm.at = small_base
            wsum, wmean, wscale = sm.take(4), sm.take(4), sm.take(4)
            amax, qs = sm.take(2 * GB), sm.take(2 * GB)
            cg, cu = sm.take(2 * GB), sm.take(2 * GB)
            hmax, hs, cd = sm.take(2), sm.take(2), sm.take(2)

            got_gu = load("load_gu", gu, io["bitgu"])
            got_dn = load("load_dn", dn, io["bitdn"])
            m = dve.do(V.memset, ones, 1.0)
            for s in range(2):
                dve.do(V.memset, hq[s][:, BI:], 0.0)
            spans = [slice(0, KT * BI), slice(KT * BI, 2 * KT * BI), slice(2 * KT * BI, 2 * KT * BI + BJ * D)]
            dve.wait(got_gu, got_dn)
            for i, sp_ in enumerate(spans):
                m = dve.do(V.tensor_reduce, wsum[:, i:i + 1], raw[:, sp_], AX.X, ALU.add, apply_absolute_value=True)
            pe.wait(m, banks[0].free)
            m = pe.do(T.matmul, banks[0].t[:, 0:3], ones, wsum[:, 0:3], start=True, stop=True)
            dve.wait(m)
            m = banks[0].free = dve.do(V.tensor_scalar, wmean[:, 0:3], banks[0].t[:, 0:3], 1.0 / (BI * D), 1e-5,
                                       ALU.mult, ALU.max)
            dve.wait(m)
            m = dve.do(V.reciprocal, wscale[:, 0:3], wmean[:, 0:3])
            dve.wait(m)
            for i, sp_ in enumerate(spans):
                m = dve.do(V.tensor_scalar, tmp[:, sp_], raw[:, sp_], wscale[:, i:i + 1], ROUND, ALU.mult, ALU.add)
                dve.wait(m)
                m = dve.do(V.tensor_scalar, tmp[:, sp_], tmp[:, sp_], ROUND, 1.0, ALU.subtract, ALU.min)
                dve.wait(m)
                wq_ready = dve.do(V.tensor_scalar, wq[:, sp_], tmp[:, sp_], -1.0, None, ALU.max)

            xq_free, xqT_free = [None] * 2, [None] * 2
            xqT_ready, scales_ready = {}, {}
            tb, hb, ob = banks[4], banks[5:7], banks[7]

            def quantise(g):
                s = g % 2
                moments(g)
                marks = normalised(g, xn)
                gs = slice(s * GB, (s + 1) * GB)
                dve.wait(*marks)
                m = dve.do(V.tensor_reduce, amax[:, gs], xn[s], AX.X, ALU.max, apply_absolute_value=True)
                dve.wait(m)
                m = dve.do(V.tensor_scalar, amax[:, gs], amax[:, gs], 1e-5, None, ALU.max)
                dve.wait(m)
                m = dve.do(V.reciprocal, qs[:, gs], amax[:, gs])
                dve.do(V.tensor_scalar, cg[:, gs], amax[:, gs], 1.0 / 127.0, wmean[:, 0:1], ALU.mult, ALU.mult)
                scales_ready[g] = dve.do(V.tensor_scalar, cu[:, gs], amax[:, gs], 1.0 / 127.0, wmean[:, 1:2],
                                         ALU.mult, ALU.mult)
                dve.wait(m)
                m = dve.do(V.tensor_scalar, qs[:, gs], qs[:, gs], 127.0, None, ALU.mult)
                dve.wait(m)
                for b in range(GB):
                    m = dve.do(V.tensor_scalar, xr[s][:, b * D:(b + 1) * D], xn[s][:, b, :],
                               qs[:, s * GB + b:s * GB + b + 1], ROUND, ALU.mult, ALU.add)
                    xn_free[s * GB + b] = m
                dve.wait(m, xq_free[s])
                m = dve.do(V.tensor_scalar, xq[s], xr[s], ROUND, None, ALU.subtract)
                pe.wait(m, tb.free, got_idb)
                tv = tb.t[:, :].bitcast(BF16)
                for k in range(KT):
                    for b in range(GB):
                        m = pe.do(T.transpose, tv[:, k * GT + b * P:k * GT + (b + 1) * P],
                                  xq[s][:, b * D + k * P:b * D + (k + 1) * P], identb[:, :])
                xq_free[s] = m
                act.wait(m, xqT_free[s])
                xqT_ready[g] = tb.free = act.do(S.copy, xqT[s], tv.rearrange("p (k t) -> p k t", k=KT))

            sg_free, hid_free, hq_free, hT_free = [None] * 2, [None] * 2, [None] * 2, [None] * 2
            HB = BI // 2
            hq_ready = {}

            def up(bb):
                g, b = divmod(bb, GB)
                s, u = g % 2, bb % 2
                pe.wait(xqT_ready[g], wq_ready)
                for i in range(4):
                    which, half = divmod(i, 2)
                    pe.wait(banks[i].free)
                    for k in range(KT):
                        m = pe.do(T.matmul, banks[i].t[:, 0:HB], xqT[s][:, k, b * P:(b + 1) * P],
                                  wgu[:, which, k, half * HB:(half + 1) * HB], start=k == 0, stop=k == KT - 1)
                    if which == 0:
                        act.wait(m, scales_ready[g], sg_free[u])
                        gated = banks[i].free = act.do(
                            S.activation, sg[u][:, half * HB:(half + 1) * HB], banks[i].t[:, 0:HB], ACT.Silu,
                            scale=cg[:, s * GB + b:s * GB + b + 1])
                    else:
                        dve.wait(m, gated, hid_free[u])
                        m_h = banks[i].free = dve.do(
                            V.scalar_tensor_tensor, out=hid[u][:, half * HB:(half + 1) * HB],
                            in0=banks[i].t[:, 0:HB], scalar=cu[:, s * GB + b:s * GB + b + 1],
                            in1=sg[u][:, half * HB:(half + 1) * HB], op0=ALU.mult, op1=ALU.mult)
                xqT_free[s] = m
                sg_free[u] = m_h
                dve.wait(m_h)
                m = dve.do(V.tensor_reduce, hmax[:, u:u + 1], hid[u], AX.X, ALU.max, apply_absolute_value=True)
                dve.wait(m)
                m = dve.do(V.tensor_scalar, hmax[:, u:u + 1], hmax[:, u:u + 1], 1e-5, None, ALU.max)
                dve.wait(m)
                m = dve.do(V.reciprocal, hs[:, u:u + 1], hmax[:, u:u + 1])
                dve.do(V.tensor_scalar, cd[:, u:u + 1], hmax[:, u:u + 1], 1.0 / 127.0, wmean[:, 2:3],
                       ALU.mult, ALU.mult)
                dve.wait(m)
                m = dve.do(V.tensor_scalar, hs[:, u:u + 1], hs[:, u:u + 1], 127.0, None, ALU.mult)
                dve.wait(m)
                m = dve.do(V.tensor_scalar, hid[u], hid[u], hs[:, u:u + 1], ROUND, ALU.mult, ALU.add)
                dve.wait(m, hq_free[u])
                hq_ready[bb] = hid_free[u] = dve.do(V.tensor_scalar, hq[u][:, 0:BI], hid[u], ROUND, None,
                                                    ALU.subtract)

            def down(bb):
                g, b = divmod(bb, GB)
                u = bb % 2
                bank = hb[u]
                pe.wait(hq_ready[bb], bank.free)
                tv = bank.t[:, :].bitcast(BF16)
                for j in range(BJ):
                    m = pe.do(T.transpose, tv[:, j * P:(j + 1) * P], hq[u][:, j * P:(j + 1) * P], identb[:, :])
                hq_free[u] = m
                act.wait(m, hT_free[u])
                m = bank.free = act.do(S.copy, hT[u], tv[:, 0:BJ * P].rearrange("p (j t) -> p j t", j=BJ))
                pe.wait(m, ob.free)
                for j in range(BJ):
                    m = pe.do(T.matmul, ob.t[:, 0:D], hT[u][:, j, :], wdn[:, j, :], start=j == 0, stop=j == BJ - 1)
                hT_free[u] = m
                dve.wait(m, x_ready[g])
                x_ready[g] = ob.free = dve.do(V.scalar_tensor_tensor, out=X[:, bb, :], in0=ob.t[:, 0:D],
                                              scalar=cd[:, u:u + 1], in1=X[:, bb, :], op0=ALU.mult, op1=ALU.add)

            quantise(0)
            for bb in range(B + 1):
                if bb < B:
                    up(bb)
                if bb % GB == 1 and bb // GB + 1 < NG:
                    quantise(bb // GB + 1)
                if bb >= 1:
                    down(bb - 1)
            phase_end()

        for n, phase in enumerate((phase1, phase2, phase3, phase4, phase5, phase6)):
            if n < phases:
                with ExitStack() as scope:
                    phase(scope)

        stored = signal("store_out")
        for g in range(NG):
            sp.wait(x_ready[g])
            m = sp.do(nc.sync.dma_start, out[:, g * GB:(g + 1) * GB, :], X[:, g * GB:(g + 1) * GB, :],
                      signal=stored, by=16)
        sp.wait(m)

        block = ctx.enter_context(nc.Block())

        @block.sync
        def _(eng):
            sp.emit()

        @block.gpsimd
        def _(eng):
            pool.emit()

        @block.scalar
        def _(eng):
            act.emit()

        @block.vector
        def _(eng):
            dve.emit()

        @block.tensor
        def _(eng):
            pe.emit()


def layouts(x, ctx_2048, mask_1xSxS2_ff0, L0_attn_W_Q, L0_attn_W_K, L0_attn_W_V, L0_attn_W_O,
            L0_attn_b_Q, L0_attn_b_K, L0_attn_b_V, L0_attn_b_O, L0_xattn_time_decay, L0_xattn_time_first,
            L0_ffn_router_w, L0_ffn_w_gate, L0_ffn_w_up, L0_ffn_w_down, L0_ffn_sh_gate, L0_ffn_sh_up,
            L0_ffn_sh_down, L0_ffn_sh_gate_w, L1_attn_g_q, L1_attn_Wq, L1_attn_bq, L1_attn_g_kv,
            L1_attn_Wkv, L1_attn_bkv, L1_attn_g_head, L1_attn_Wo, L1_attn_bo, L1_xattn_Wq, L1_xattn_bq,
            L1_xattn_Wk, L1_xattn_bk, L1_xattn_Wv, L1_xattn_bv, L1_xattn_Wo, L1_xattn_qn_w,
            L1_xattn_kn_w, L1_ffn_w_gate, L1_ffn_w_up, L1_ffn_w_down):
    f = np.float32
    bf = mybir.dt.np(BF16)
    a = {}
    a["x"] = x.transpose(1, 0, 2)
    a["ctxT"] = ctx_2048.reshape(NT, KT, P).transpose(2, 1, 0)
    a["mask"] = mask_1xSxS2_ff0[0]
    a["ident"] = np.eye(P, dtype=f)
    a["identb"] = np.eye(P, dtype=f).astype(bf)
    a["causal"] = np.where(np.tril(np.ones((P, P), bool)), 0.0, NEG).astype(f)

    def columns(v):
        return v.reshape(-1, P).T
    vec = [L0_attn_b_Q.T, L0_attn_b_K.T, columns(L0_xattn_time_decay), columns(L0_xattn_time_first),
           columns(L1_attn_g_q), columns(L1_attn_g_kv), np.tile(L1_attn_g_head, P // DS)[:, None],
           columns(L1_xattn_bq), L1_xattn_qn_w[:, None], L1_xattn_kn_w[:, None]]
    vec = np.concatenate(vec, 1)
    a["vec"] = np.concatenate([vec, np.zeros((P, 64 - vec.shape[1]), f)], 1)

    w = np.stack([L0_attn_W_Q, L0_attn_W_K, L0_attn_W_V])
    w = w.reshape(3, NHG, HG, KT, P, DH).transpose(4, 1, 0, 3, 2, 5)
    a["wqkv0"] = w.reshape(P, NHG, 3 * KT * HG * DH)
    a["wo0"] = L0_attn_W_O.reshape(NHG, HG, DH, D).transpose(2, 0, 1, 3)
    a["bv0"] = L0_attn_b_V.reshape(-1)
    a["bo0"] = L0_attn_b_O

    def hidden(w, shared):
        w = np.concatenate([w.transpose(1, 0, 2).reshape(D, E * EI), shared], 1)
        return np.concatenate([w, np.zeros((D, NJ * P - HID), f)], 1).reshape(KT, P, NJ, P)
    gate, up = hidden(L0_ffn_w_gate, L0_ffn_sh_gate), hidden(L0_ffn_w_up, L0_ffn_sh_up)
    down = np.concatenate([L0_ffn_w_down.reshape(E * EI, D), L0_ffn_sh_down, np.zeros((NJ * P - HID, D), f)])
    moe = np.concatenate([gate.transpose(1, 2, 0, 3).reshape(P, NJ, D), up.transpose(1, 2, 0, 3).reshape(P, NJ, D),
                          down.reshape(NJ, P, D).transpose(1, 0, 2)], 2)
    a["moe"] = moe
    r = np.concatenate([L0_ffn_router_w.T, L0_ffn_sh_gate_w, np.zeros((D, P - CW), f)], 1)
    a["router"] = r.reshape(KT, P, P).transpose(1, 0, 2)
    owner = np.minimum(np.arange(NJ * P) // EI, E)
    one = (owner[None, :] == np.arange(CW)[:, None]).astype(f)
    a["sel"] = np.concatenate([one] * NSPLIT + [np.zeros((P - NSPLIT * CW, NJ * P), f)]).astype(bf)

    w = np.concatenate([L1_attn_Wq, L1_attn_Wkv], 1)
    a["wqkv1"] = w.reshape(KT, P, 3 * D).transpose(1, 0, 2)
    a["wo1"] = L1_attn_Wo.reshape(KT, P, D).transpose(1, 0, 2)
    a["bqkv1"] = np.concatenate([L1_attn_bq, L1_attn_bkv])
    a["bo1"] = L1_attn_bo
    a["mask8"] = (np.arange(P)[:, None] // DS == np.arange(8)[None, :]).astype(f)

    a["wkvx"] = np.concatenate([L1_xattn_Wk, L1_xattn_Wv], 1).reshape(KT, P, 2 * 512).transpose(1, 0, 2)
    a["bkvx"] = np.concatenate([L1_xattn_bk, L1_xattn_bv])
    a["wqx"] = L1_xattn_Wq.reshape(KT, P, NHG, HG * DH).transpose(1, 2, 0, 3)
    a["wox"] = L1_xattn_Wo.reshape(NHG, HG, DH, D).transpose(2, 0, 1, 3)

    gu = np.stack([L1_ffn_w_gate, L1_ffn_w_up])
    a["bitgu"] = gu.reshape(2, BI, KT, P).transpose(3, 0, 2, 1).reshape(P, 2 * KT * BI)
    dn = np.concatenate([L1_ffn_w_down.T, np.zeros((BJ * P - BI, D), f)])
    a["bitdn"] = dn.reshape(BJ, P, D).transpose(1, 0, 2).reshape(P, BJ * D)
    return {k: np.ascontiguousarray(v) for k, v in a.items()}


def program(nc, arrays, phases=6):
    io = {n: nc.dram_tensor(f"in_{n}", v.shape, mybir.dt.from_np(v.dtype), kind="ExternalInput").ap()
          for n, v in arrays.items()}
    out = nc.dram_tensor("out_x", (P, B, D), F32, kind="ExternalOutput").ap()
    build(nc, io, out, phases)


def kernel(**inputs):
    import concourse.bacc as bacc
    from concourse.bass_utils import run_bass_kernel_spmd

    arrays = layouts(**{k: np.asarray(v) for k, v in inputs.items()})
    nc = bacc.Bacc("TRN2", target_bir_lowering=False, num_devices=1)
    program(nc, arrays)
    r = run_bass_kernel_spmd(nc, [{f"in_{n}": v for n, v in arrays.items()}], core_ids=[0])
    return np.ascontiguousarray(r.results[0]["out_x"].transpose(1, 0, 2))
```

```python
from contextlib import ExitStack

import numpy as np

import concourse.bass as bass
from concourse import mybir

F32 = mybir.dt.float32
F32R = mybir.dt.float32r
BF16 = mybir.dt.bfloat16
ALU = mybir.AluOpType
ACT = mybir.ActivationFunctionType
AX = mybir.AxisListType

P = 128
B = 16
D = 256
KT = D // P
GB = 4
NG = B // GB
GT = GB * P
NT = B * P
H = 16
HG = 4
NHG = H // HG
DH = 128
DS = D // H
NKV = 4
E = 16
EI = 176
SI = 704
TOPK = 4
HID = E * EI + SI
NJ = -(-HID // P)
JW = 6 * P
BI = 832
BJ = -(-BI // P)
NSPLIT = 3
CW = E + 1
ROUND = 12582912.0
LN_EPS = 1e-5
RMS_EPS = float(np.finfo(np.float32).eps)
QK_EPS = 1e-6
SBUF_COLUMNS = 35584
KEPT_COLUMNS = NT // 2 + GT + 2 * KT * P
FAR_COLUMNS = 9216
SMALL_COLUMNS = 968
NEG = -1e30
SEG = P + 1


class Signal:

    def __init__(self, sem):
        self.sem, self.count = sem, 0


class Queue:

    def __init__(self, wait_ge, own):
        self.steps, self.passed, self.wait_ge, self.own = [], {}, wait_ge, own
        self.mark = None

    def wait(self, *marks):
        for m in marks:
            if m is not None and self.passed.get(m[0], 0) < m[1]:
                self.passed[m[0]] = m[1]
                self.steps.append((self.wait_ge, (m[0].sem, m[1]), {}, None, 0))

    def do(self, method, *args, signal=None, by=1, **kw):
        signal = signal or self.own
        signal.count += by
        self.steps.append((method, args, kw, signal.sem, by))
        if by == 1:
            self.mark = (signal, signal.count)
        return (signal, signal.count)

    def quiet(self, method, *args, **kw):
        self.steps.append((method, args, kw, None, 0))

    def emit(self):
        for method, args, kw, sem, by in self.steps:
            made = method(*args, **kw)
            if sem is not None:
                made.then_inc(sem, by)


class Bank:

    def __init__(self, tensor):
        self.t, self.free = tensor, None


def build(nc, io, out, phases=6):
    with ExitStack() as ctx:
        def sb(name, shape, dt=F32):
            return ctx.enter_context(nc.sbuf_tensor(name, shape, dt))

        def signal(name):
            return Signal(ctx.enter_context(nc.semaphore(name)))

        pe = Queue(nc.tensor.wait_ge, signal("pe_steps"))
        dve = Queue(nc.vector.wait_ge, signal("dve_steps"))
        act = Queue(nc.scalar.wait_ge, signal("act_steps"))
        pool = Queue(nc.gpsimd.wait_ge, signal("pool_steps"))
        sp = Queue(nc.sync.wait_ge, signal("sp_unused"))
        V, S, G, T = nc.vector, nc.scalar, nc.gpsimd, nc.tensor

        def load(name, dst, src):
            return sp.do(nc.sync.dma_start, dst, src, signal=signal(name), by=16)

        def phase_end():
            marks = [q.mark for q in (pe, dve, act, pool)]
            for q in (pe, dve, act, pool, sp):
                q.wait(*marks)

        X = sb("residual", [P, B, D])
        XT = sb("x_channel_major", [P, 2, KT, NT], F32R)
        ident = sb("identity", [P, P])
        identb = sb("identity_bf16", [P, P], BF16)
        vec = sb("channel_vectors", [P, 64])
        wkv_w = sb("wkv_decay", [P, KT])[:, :]
        small = sb("small", [P, SMALL_COLUMNS])
        xn_kept = sb("normalised_tiles", [P, 2 * GB * D])
        tiles_xn = [xn_kept[:, s * GB * D:(s + 1) * GB * D].rearrange("p (b d) -> p b d", b=GB) for s in range(2)]
        banks = [Bank(ctx.enter_context(nc.psum_tensor(f"bank{i}", [P, 512], F32))) for i in range(8)]

        class Carve:

            def __init__(self, t, width):
                self.t, self.width, self.at = t, width, 0

            def take(self, n):
                n += n % 2
                a = self.t[:, self.at:self.at + n]
                self.at += n
                assert self.at <= self.width, (self.at, self.width)
                return a

        got_x = load("load_x0", X[:, 0:GB, :], io["x"][:, 0:GB, :])
        got_id = load("load_ident", ident[:, :], io["ident"])
        got_idb = load("load_identb", identb[:, :], io["identb"])
        got_vec = load("load_vec", vec[:, :], io["vec"])
        x_ready = {0: got_x}

        kept = ExitStack()

        def keep(name, shape, dt=F32):
            return kept.enter_context(nc.sbuf_tensor(name, shape, dt))

        combT = keep("combine_weights", [P, NT], BF16)
        lt = keep("router_logits", [P, GT])[:, :]
        router = [keep(f"router_{part}", [P, KT, P], F32R)[:, :, :] for part in ("hi", "lo")]

        def columns(scope, name, n, dt=F32, side=None):
            t = scope.enter_context(nc.sbuf_tensor(name, [P, n], dt, **({"side": side} if side else {})))
            return Carve(t, n)

        def slack(n):
            for _ in range(n):
                yield

        class Spread:

            def __init__(self):
                self.work = []

            def add(self, *gens):
                self.work += gens

            def step(self, n=1):
                for _ in range(n):
                    while self.work and next(self.work[0], "done") == "done":
                        self.work.pop(0)

            def finish(self):
                while self.work:
                    self.step()

        side_work = Spread()
        right = ctx.enter_context(ExitStack())

        sm = Carve(small, SMALL_COLUMNS)
        eps_ln, eps_rms, eps_qk, eps_both = (sm.take(2) for _ in range(4))
        dve.do(V.memset, eps_ln[:, 0:1], LN_EPS)
        dve.do(V.memset, eps_rms[:, 0:1], RMS_EPS)
        dve.do(V.memset, eps_both[:, 0:1], RMS_EPS * LN_EPS)
        got_eps = dve.do(V.memset, eps_qk[:, 0:1], QK_EPS)
        stats = sm.take(GB * 6 * 2).rearrange("p (s b c) -> p s b c", s=2, b=GB)
        mv = sm.take(GB * 2 * 2).rearrange("p (s b c) -> p s b c", s=2, b=GB)
        sd = sm.take(GB * 2).rearrange("p (s b) -> p s b", s=2)
        rstd = sm.take(GB * 2).rearrange("p (s b) -> p s b", s=2)

        def matmul3(out_ap, w_hi, w_lo, x_hi, x_lo, first, last):
            pe.quiet(T.matmul, out_ap, w_hi, x_hi, start=first, stop=False)
            pe.quiet(T.matmul, out_ap, w_hi, x_lo, start=False, stop=False)
            if last:
                return pe.do(T.matmul, out_ap, w_lo, x_hi, start=False, stop=True)
            pe.quiet(T.matmul, out_ap, w_lo, x_hi, start=False, stop=False)

        def project(bank, pairs):
            pe.wait(bank.free)
            m = None
            for i, (w_hi, w_lo, x_hi, x_lo) in enumerate(pairs):
                m = matmul3(bank.t[:, 0:x_hi.shape[-1]], w_hi, w_lo, x_hi, x_lo, i == 0, i == len(pairs) - 1)
            return m

        def split(hi, lo, src, ready, hi_q, hi_op, lo_q, lo_op, kw=None):
            hi_q.wait(*ready)
            a = hi_q.do(hi_op, hi, src, **(kw or {}))
            lo_q.wait(a, *ready)
            return lo_q.do(lo_op, lo, src, hi.bitcast(F32), ALU.subtract)

        xn_free = [None] * 8
        sd_ready = {}

        def moments(g, then_rms=False):
            s = g % 2
            dve.wait(x_ready[g])
            for b in range(GB):
                m = dve.do(V.bn_stats, stats[:, s, b, :], X[:, g * GB + b, :])
            dve.wait(m)
            for b in range(GB):
                m = dve.do(V.bn_aggr, mv[:, s, b, :], stats[:, s, b, :])
            act.wait(m, got_eps)
            eps, scale = (eps_both, 1.0 + RMS_EPS) if then_rms else (eps_ln, 1.0)
            sd_ready[g] = act.do(S.activation, sd[:, s, :], mv[:, s, :, 1], ACT.Sqrt, bias=eps[:, 0:1], scale=scale)

        def normalised(g, xn):
            s = g % 2
            dve.wait(sd_ready[g])
            m = dve.do(V.reciprocal, rstd[:, s, :], sd[:, s, :])
            dve.wait(m)
            marks = []
            for b in range(GB):
                dve.wait(xn_free[s * GB + b])
                marks.append(dve.do(V.tensor_scalar, xn[s][:, b, :], X[:, g * GB + b, :], mv[:, s, b, 0:1],
                                    rstd[:, s, b:b + 1], ALU.subtract, ALU.mult))
            return marks

        def to_channels(g, xn, marks, kt, bank):
            s = g % 2
            pe.wait(bank.free, got_id)
            for b in range(GB):
                pe.wait(marks[b])
                m = pe.do(T.transpose, bank.t[:, b * P:(b + 1) * P], xn[s][:, b, kt * P:(kt + 1) * P],
                          ident[:, :])
                if kt == KT - 1:
                    xn_free[s * GB + b] = m
            return m

        def split_channels(g, xn, marks, kt, bank):
            done = to_channels(g, xn, marks, kt, bank)
            sl = slice(g * GT, (g + 1) * GT)
            bank.free = split(XT[:, 0, kt, sl], XT[:, 1, kt, sl], bank.t[:, :], [done],
                              act, S.copy, dve, V.tensor_tensor)
            return bank.free

        second_xt, second_tiles, next_weights = {}, {}, []

        def second_norm(g):
            moments(g, then_rms=True)
            yield
            second_tiles[g] = marks = normalised(g, tiles_xn)
            yield
            yield
            for kt in range(KT):
                second_xt[g] = split_channels(g, tiles_xn, marks, kt, side_work.next_bank())
                yield

        def four(ap):
            return ap.rearrange("p (h k) -> p h k", h=HG)

        def row_max(negmax, scores_in, ready):
            dve.wait(ready)
            return dve.do(V.tensor_reduce, negmax, scores_in, AX.X, ALU.max, negate=True)

        def exponentials(probs, scores_in, negmax, sums, ready, free):
            act.wait(ready, free)
            for h in range(HG):
                m = act.do(S.activation, probs[:, h, :], scores_in[:, h, :], ACT.Exp, bias=negmax[:, h:h + 1],
                           accum_out=sums[:, h:h + 1])
            return m

        def normalise(probs, sums, rinv, ready):
            dve.wait(ready)
            m = dve.do(V.reciprocal, rinv, sums)
            dve.wait(m)
            return dve.do(V.tensor_tensor, probs, probs, rinv.unsqueeze(2).broadcast_to([P, HG, P]), ALU.mult)

        def self_attention(scope):
            WS = 3 * KT * HG * DH
            wr = columns(scope, "qkv_weights_split_odd", 2 * WS, F32R)
            ar = columns(scope, "self_attention", SBUF_COLUMNS - FAR_COLUMNS - 2 * WS)
            far = ExitStack()
            wr_even = columns(far, "qkv_weights_split_even", 2 * WS, F32R, "right")
            raw = columns(far, "qkv_weights_raw", WS, F32, "right").take(WS)
            wo = [ar.take(HG * D).rearrange("p (h d) -> p h d", h=HG) for _ in range(2)]
            qT = [ar.take(HG * GT).rearrange("p (h t) -> p h t", h=HG) for _ in range(2)]
            kT = [ar.take(HG * GT).rearrange("p (h t) -> p h t", h=HG) for _ in range(2)]
            vv = [ar.take(GB * HG * DH).rearrange("p (b c) -> p b c", b=GB) for _ in range(2)]
            Smask = [ar.take(512).rearrange("p (h k) -> p h k", h=HG) for _ in range(2)]
            Pm = [ar.take(512).rearrange("p (h k) -> p h k", h=HG) for _ in range(2)]
            PT = [ar.take(512).rearrange("p (h k) -> p h k", h=HG) for _ in range(2)]
            ZT = [ar.take(512).rearrange("p (h k) -> p h k", h=HG) for _ in range(2)]
            bvb = [ar.take(HG * DH) for _ in range(2)]
            xn = tiles_xn
            bob = ar.take(D)
            causal = ar.take(P)
            sm.at = small_base
            negmax = [sm.take(HG) for _ in range(2)]
            sums = [sm.take(HG) for _ in range(2)]
            rinv = [sm.take(HG) for _ in range(2)]
            bqs = sm.take(H)
            scale = 1.0 / float(np.sqrt(np.float32(DH)))

            wr = [[carve.take(WS).rearrange("p (m k c) -> p m k c", m=3, k=KT) for part in range(2)]
                  for carve in (wr_even, wr)]
            raw_v = raw.rearrange("p (m k c) -> p m k c", m=3, k=KT)

            weights_ready, wo_ready, bv_ready = {}, {}, {}
            bv_free = [None, None]
            raw_free = [None]
            wr_free = [None, None]
            wo_free = [None, None]

            def fetch_weights(hg, meanwhile=lambda: None):
                s = hg % 2
                sp.wait(raw_free[0], wo_free[s])
                third = WS // 3
                got = [load(f"load_wqkv{hg}_{m}", raw[:, m * third:(m + 1) * third],
                            io["wqkv0"][:, hg, m * third:(m + 1) * third]) for m in range(3)]
                wo_ready[hg] = load(f"load_wo{hg}", wo[s], io["wo0"][:, hg])
                sp.wait(bv_free[s])
                bv_ready[hg] = load(f"load_bv{hg}", bvb[s],
                                    io["bv0"][hg * HG * DH:(hg + 1) * HG * DH].partition_broadcast(P))
                meanwhile()
                marks = []
                for m in range(3):
                    hq, hop, lq, lop = (act, S.copy, dve, V.tensor_tensor) if hg == 0 else \
                                       (pool, G.tensor_copy, pool, G.tensor_tensor)
                    marks.append(split(wr[s][0][:, m], wr[s][1][:, m], raw_v[:, m], [got[m], wr_free[s]],
                                       hq, hop, lq, lop))
                weights_ready[hg] = marks
                raw_free[0] = marks[-1]

            xt_ready, bo_added = {}, {}

            def first_norm(g):
                moments(g)
                yield
                marks = normalised(g, xn)
                yield
                for kt in range(KT):
                    m = split_channels(g, xn, marks, kt, side_work.next_bank())
                    yield
                xt_ready[g] = m
                yield
                dve.wait(got_bo)
                for b in range(GB):
                    bo_added[g] = dve.do(V.tensor_tensor, X[:, g * GB + b, :], X[:, g * GB + b, :], bob, ALU.add)
                yield

            side_work.next_bank = lambda: banks[5]
            side_work.add(first_norm(0))
            side_work.step()

            def first_group():
                while 0 not in xt_ready:
                    side_work.step()

            fetch_weights(0, first_group)
            got_causal = load("load_causal", causal, io["causal"])
            for g in range(1, NG):
                x_ready[g] = load(f"load_x{g}", X[:, g * GB:(g + 1) * GB, :], io["x"][:, g * GB:(g + 1) * GB, :])
            got_bo = load("load_bo", bob, io["bo0"].partition_broadcast(P))
            load_router()
            side_work.add(*(first_norm(g) for g in range(1, NG)))
            act.wait(got_vec)
            got_bqs = act.do(S.mul, bqs, vec[:, 0:H], scale)

            fill_banks = banks[0:2]
            nfill = [0]
            q_ready, k_ready, v_ready = {}, {}, {}
            qk_free = [None, None]
            v_free = [None, None]

            def fill(grp, i):
                hg, g = divmod(grp, NG)
                s, ws = grp % 2, hg % 2
                bank = fill_banks[nfill[0] % 2]
                nfill[0] += 1
                hi, lo = wr[ws]
                pe.wait(weights_ready[hg][i // HG], xt_ready[g])
                if i < 8:
                    m, h = divmod(i, HG)
                    cs, ts = slice(h * DH, (h + 1) * DH), slice(g * GT, (g + 1) * GT)
                    done = project(bank, [(hi[:, m, k, cs], lo[:, m, k, cs], XT[:, 0, k, ts], XT[:, 1, k, ts])
                                          for k in range(KT)])
                    act.wait(done, qk_free[s], got_bqs)
                    hh = hg * HG + h
                    if m == 0:
                        r = act.do(S.activation, qT[s][:, h, :], bank.t[:, :], ACT.Identity,
                                   bias=bqs[:, hh:hh + 1], scale=scale)
                        q_ready[grp] = r
                    else:
                        r = act.do(S.activation, kT[s][:, h, :], bank.t[:, :], ACT.Identity,
                                   bias=vec[:, H + hh:H + hh + 1])
                        k_ready[grp] = r
                else:
                    b = i - 8
                    ts = slice((g * GB + b) * P, (g * GB + b + 1) * P)
                    done = project(bank, [(XT[:, 0, k, ts], XT[:, 1, k, ts], hi[:, 2, k, :], lo[:, 2, k, :])
                                          for k in range(KT)])
                    dve.wait(done, v_free[s], bv_ready[hg])
                    r = bv_free[ws] = dve.do(V.tensor_tensor, vv[s][:, b, :], bank.t[:, :], bvb[ws], ALU.add)
                    v_ready[grp, b] = r
                bank.free = r
                wr_free[ws] = done

            sbank, tbank, zbank, obank = banks[2:4], banks[4], banks[6], banks[7]
            max_ready, exp_ready, probs_ready, pt_ready, z_ready = {}, {}, {}, {}, {}
            Sm_free, P_free, PT_free, ZT_free = [None] * 2, [None] * 2, [None] * 2, [None] * 2

            def scores(n):
                grp, b = divmod(n, GB)
                s, u = grp % 2, n % 2
                bank = sbank[u]
                pe.wait(bank.free, q_ready[grp], k_ready[grp])
                ts = slice(b * P, (b + 1) * P)
                for h in range(HG):
                    m = pe.do(T.matmul, bank.t[:, h * P:(h + 1) * P], qT[s][:, h, ts], kT[s][:, h, ts],
                              start=True, stop=True)
                qk_free[s] = m
                dve.wait(m, Sm_free[u], got_causal)
                m = bank.free = dve.do(V.tensor_tensor, Smask[u], four(bank.t[:, :]),
                                       causal.unsqueeze(1).broadcast_to([P, HG, P]), ALU.add)
                max_ready[n] = row_max(negmax[u], Smask[u], m)

            def exps(n):
                u = n % 2
                exp_ready[n] = Sm_free[u] = exponentials(Pm[u], Smask[u], negmax[u], sums[u], max_ready[n],
                                                         P_free[u])

            def norm(n):
                u = n % 2
                probs_ready[n] = normalise(Pm[u], sums[u], rinv[u], exp_ready[n])

            def transposes(n):
                u, bank = n % 2, tbank
                pe.wait(bank.free, probs_ready[n])
                for h in range(HG):
                    m = pe.do(T.transpose, bank.t[:, h * P:(h + 1) * P], Pm[u][:, h, :], ident[:, :])
                P_free[u] = m
                act.wait(m, PT_free[u])
                pt_ready[n] = bank.free = act.do(S.copy, PT[u], four(bank.t[:, :]))

            def values(n):
                grp, b = divmod(n, GB)
                s, u = grp % 2, n % 2
                pe.wait(zbank.free, pt_ready[n], v_ready[grp, b])
                for h in range(HG):
                    m = pe.do(T.matmul, zbank.t[:, h * P:(h + 1) * P], vv[s][:, b, h * DH:(h + 1) * DH],
                              PT[u][:, h, :], start=True, stop=True)
                PT_free[u] = m
                v_free[s] = m
                dve.wait(m, ZT_free[u])
                z_ready[n] = zbank.free = dve.do(V.tensor_copy, ZT[u], four(zbank.t[:, :]))

            def output(n):
                grp, b = divmod(n, GB)
                hg, g = divmod(grp, NG)
                u = n % 2
                pe.wait(obank.free, z_ready[n], wo_ready[hg])
                for h in range(HG):
                    m = pe.do(T.matmul, obank.t[:, 0:D], ZT[u][:, h, :], wo[hg % 2][:, h, :],
                              start=h == 0, stop=h == HG - 1)
                ZT_free[u] = m
                wo_free[hg % 2] = m
                dve.wait(m, bo_added[g], x_ready[g])
                x_ready[g] = obank.free = dve.do(V.tensor_tensor, X[:, g * GB + b, :], obank.t[:, 0:D],
                                                 X[:, g * GB + b, :], ALU.add)

            for i in range(12):
                fill(0, i)
                side_work.step()
            fetch_weights(1)
            nsteps = NHG * NG * GB
            LAST = (NHG - 1) * NG * GB
            for n in range(nsteps + 1):
                grp, b = divmod(n, GB)
                nxt = grp + 1
                more = nxt < NHG * NG and n < nsteps
                if n == LAST:
                    far_free = [pool.mark, act.mark, dve.mark, pe.mark]
                    far.close()
                    wkv.open(far_free)
                if n > LAST and (n - LAST) % GB == 1 and n - LAST > GB:
                    done = (n - LAST) // GB - 1
                    if done == 0:
                        side_work.add(wkv.group(0), routing(0))
                    elif done == 1:
                        side_work.add(wkv.group(1))
                if n < nsteps:
                    scores(n)
                side_work.step()
                if n >= 1:
                    transposes(n - 1)
                if n < nsteps:
                    exps(n)
                side_work.step()
                if more:
                    fill(nxt, 3 * b)
                if n >= 1:
                    values(n - 1)
                side_work.step()
                if more:
                    fill(nxt, 3 * b + 1)
                if n < nsteps:
                    norm(n)
                side_work.step()
                if n >= 1:
                    output(n - 1)
                side_work.step()
                if more:
                    fill(nxt, 3 * b + 2)
                side_work.step()
                if b == 0 and grp % NG == 0 and 0 < grp // NG < NHG - 1:
                    fetch_weights(grp // NG + 1)
            phase_end()

        class Wkv:

            def open(self, free):
                for q in (pe, dve, act, pool, sp):
                    q.wait(*free)
                ar = columns(right, "wkv", FAR_COLUMNS, F32, "right")

                def seg():
                    return ar.take(GB * SEG).rearrange("p (b t) -> p b t", b=GB)

                def flat():
                    return ar.take(GT).rearrange("p (b t) -> p b t", b=GB)
                self.key, self.peak, self.num, self.den = seg(), seg(), seg(), seg()
                self.e2v, self.e2b, self.e1b = seg(), seg(), seg()
                self.decay = [seg() for _ in range(KT)]
                self.q, self.e1, self.e2, self.t1, self.t2, self.y = (flat() for _ in range(6))
                self.value = [flat() for _ in range(2)]
                self.value_free = [None] * 2
                self.nchunk = 0
                self.last = self.helped = None
                side_work.next_bank = lambda: banks[5]
                act.wait(got_vec)
                m = act.do(S.activation, wkv_w, vec[:, 32:34], ACT.Exp)
                dve.wait(m)
                m = dve.do(V.tensor_scalar, wkv_w, wkv_w, -1.0, None, ALU.mult)
                dve.wait(m)
                for kt in range(KT):
                    m = dve.do(V.memset, self.decay[kt], 0.0)
                    dve.wait(m)
                    m = dve.do(V.tensor_scalar, self.decay[kt], self.decay[kt], wkv_w[:, kt:kt + 1], None, ALU.add)
                    dve.wait(m)
                    dve.do(V.memset, self.decay[kt][:, :, 0:1], -1e38)
                dve.do(V.memset, self.key[:, :, 0:1], -1e38)
                for a in (self.e1b, self.e2v, self.e2b):
                    m = dve.do(V.memset, a[:, :, 0:1], 0.0)
                dve.wait(m)
                self.init = m

            def group(self, g):
                xn = tiles_xn
                moments(g)
                yield
                marks = normalised(g, xn)
                yield
                yield
                for kt in range(KT):
                    yield from self.chunk(g, kt, marks, xn)

            def chunk(self, g, kt, marks, xn):
                now, was = slice(1, SEG), slice(0, P)
                s = self.nchunk % 2
                self.nchunk += 1
                key, peak, num, den = self.key, self.peak, self.num, self.den
                e2v, e2b, e1b, q, e1, e2 = self.e2v, self.e2b, self.e1b, self.q, self.e1, self.e2
                t1, t2, y, v = self.t1, self.t2, self.y, self.value[s]
                decay, w, u = self.decay[kt], wkv_w[:, kt:kt + 1], vec[:, 34 + kt:35 + kt]
                line = "p b t -> p (b t)"
                sp.wait(self.value_free[s])
                got_v = load(f"load_value{g}_{kt}", v.rearrange(line), io["ctxT"][:, kt, g * GT:(g + 1) * GT])
                bank = side_work.next_bank()
                done = to_channels(g, xn, marks, kt, bank)
                yield
                act.wait(done, self.init, self.last)
                m = bank.free = act.do(S.copy, key[:, :, now], bank.t[:, :].rearrange("p (b t) -> p b t", b=GB))
                k = key[:, :, now]
                yield
                dve.wait(m)
                m = dve.do(V.tensor_tensor_scan, peak.rearrange(line), decay.rearrange(line), key.rearrange(line),
                           -1e38, ALU.add, ALU.max)
                dve.wait(m)
                yield
                dve.do(V.scalar_tensor_tensor, out=e1b[:, :, now], in0=peak[:, :, was], scalar=w,
                       in1=peak[:, :, now], op0=ALU.add, op1=ALU.subtract)
                x = dve.do(V.tensor_tensor, e2b[:, :, now], k, peak[:, :, now], ALU.subtract)
                yield
                act.wait(x)
                for a in (e2b[:, :, now], e1b[:, :, now]):
                    act.do(S.activation, a, a, ACT.Exp)
                m = dve.do(V.scalar_tensor_tensor, out=q, in0=k, scalar=u, in1=peak[:, :, was],
                           op0=ALU.add, op1=ALU.max)
                dve.wait(m)
                dve.do(V.tensor_tensor, e1, peak[:, :, was], q, ALU.subtract)
                yield
                m = dve.do(V.scalar_tensor_tensor, out=e2, in0=k, scalar=u, in1=q, op0=ALU.add, op1=ALU.subtract)
                act.wait(m)
                for a in (e2, e1):
                    x = act.do(S.activation, a, a, ACT.Exp)
                yield from slack(1 if g < 2 else 2)
                helper, ops = (pool, G) if g < 2 else (dve, V)
                helper.wait(x, got_v, self.helped)
                pv = helper.do(ops.tensor_tensor, e2v[:, :, now], e2b[:, :, now], v, ALU.mult)
                self.value_free[s] = p2 = helper.do(ops.tensor_tensor, t2, e2, v, ALU.mult)
                dve.wait(x)
                yield
                mb = dve.do(V.tensor_tensor_scan, den.rearrange(line), e1b.rearrange(line), e2b.rearrange(line),
                            0.0, ALU.mult, ALU.add)
                yield
                dve.wait(mb)
                m = dve.do(V.tensor_tensor, t1, e1, den[:, :, was], ALU.mult)
                dve.wait(m)
                m = dve.do(V.tensor_tensor, t1, t1, e2, ALU.add)
                yield
                dve.wait(pv)
                ma = dve.do(V.tensor_tensor_scan, num.rearrange(line), e1b.rearrange(line), e2v.rearrange(line),
                            0.0, ALU.mult, ALU.add)
                yield
                dve.wait(m)
                for half in range(2):
                    hs = slice(half * GB // 2, (half + 1) * GB // 2)
                    m = dve.do(V.reciprocal, t1[:, hs], t1[:, hs])
                    yield
                dve.wait(ma)
                m2 = dve.do(V.tensor_tensor, q, e1, num[:, :, was], ALU.mult)
                dve.wait(p2, m2)
                m2 = dve.do(V.tensor_tensor, t2, t2, q, ALU.add)
                yield
                dve.wait(m, m2)
                m = dve.do(V.tensor_tensor, y, t1, t2, ALU.mult)
                yield from slack(2 if g < 2 else 3)
                bank = side_work.next_bank()
                pe.wait(m, bank.free)
                for b in range(GB):
                    m = pe.do(T.transpose, bank.t[:, b * P:(b + 1) * P], y[:, b, :], ident[:, :])
                self.last = m
                self.helped = m
                yield
                dve.wait(m)
                xs = X[:, g * GB:(g + 1) * GB, kt * P:(kt + 1) * P]
                bank.free = x_ready[g] = dve.do(V.tensor_tensor, xs, bank.t[:, :].rearrange("p (b t) -> p b t", b=GB),
                                                xs, ALU.add)
                yield

        wkv = Wkv()

        L = sm.take(GB * CW).rearrange("p (b c) -> p b c", b=GB)
        nm, zs, rz, s4, r4, sg = (sm.take(GB) for _ in range(6))
        PR = sm.take(GB * (TOPK + E)).rearrange("p (b c) -> p b c", b=GB)
        MR = sm.take(GB * (TOPK + E)).rearrange("p (b c) -> p b c", b=GB)
        top = sm.take(GB * 8).rearrange("p (b c) -> p b c", b=GB)
        C = sm.take(GB * CW).rearrange("p (b c) -> p b c", b=GB)
        CS = sm.take(GB * 64 // 2).bitcast(BF16).rearrange("p (b c) -> p b c", b=GB)
        rest = sm.take(GB * CW).rearrange("p (b c) -> p b c", b=GB)
        m = dve.do(V.memset, PR[:, :, 0:TOPK], 2.0)
        dve.do(V.memset, combT[:, :], 0.0)

        wsum, wmean, wscale = sm.take(8), sm.take(4), sm.take(4)
        step_x, per_x, worth_gate, worth_up = (sm.take(B) for _ in range(4))
        small_base = sm.at
        comb_ready = {}
        rt_free = [None]
        router_ready = []

        def load_router():
            rraw = lt[:, 0:KT * P].rearrange("p (k c) -> p k c", k=KT)
            got_router = load("load_router", rraw, io["router"])
            done = split(router[0], router[1], rraw, [got_router], pool, G.tensor_copy, pool, G.tensor_tensor)
            router_ready.append(done)
            rt_free[0] = done

        def routing(g):
            moments(g)
            yield
            marks = normalised(g, tiles_xn)
            yield
            yield
            for kt in range(KT):
                xt_ready = split_channels(g, tiles_xn, marks, kt, side_work.next_bank())
                yield
            pe.wait(xt_ready, *router_ready)
            lb = side_work.next_bank()
            ts = slice(g * GT, (g + 1) * GT)
            done = project(lb, [(router[0][:, k, :], router[1][:, k, :], XT[:, 0, k, ts], XT[:, 1, k, ts])
                                      for k in range(KT)])
            act.wait(done, rt_free[0])
            m = lb.free = act.do(S.copy, lt[0:32, :], lb.t[0:32, :])
            yield
            tb = side_work.next_bank()
            pe.wait(m, tb.free)
            for b in range(GB):
                m = pe.do(T.transpose, tb.t[:, b * 32:(b + 1) * 32], lt[0:32, b * P:(b + 1) * P],
                          ident[0:32, 0:32])
            rt_free[0] = m
            yield
            dve.wait(m)
            bt = tb.t[:, 0:GB * 32].rearrange("p (b c) -> p b c", b=GB)
            m = tb.free = dve.do(V.tensor_copy, L, bt[:, :, 0:CW])
            dve.wait(m)
            m = dve.do(V.tensor_reduce, nm, L[:, :, 0:E], AX.X, ALU.max)
            yield
            dve.wait(m)
            m = dve.do(V.tensor_tensor, L[:, :, 0:E], L[:, :, 0:E], nm.unsqueeze(2).broadcast_to([P, GB, E]),
                       ALU.subtract)
            act.wait(m)
            m = act.do(S.activation, L[:, :, 0:E], L[:, :, 0:E], ACT.Exp)
            msg = act.do(S.activation, sg, L[:, :, E], ACT.Exp, scale=-1.0)
            yield
            dve.wait(m)
            m = dve.do(V.tensor_reduce, zs, L[:, :, 0:E], AX.X, ALU.add)
            dve.wait(m)
            m = dve.do(V.reciprocal, rz, zs)
            yield
            dve.wait(m, msg)
            m = dve.do(V.tensor_tensor, PR[:, :, TOPK:], L[:, :, 0:E], rz.unsqueeze(2).broadcast_to([P, GB, E]),
                       ALU.mult)
            msg = dve.do(V.tensor_scalar, sg, sg, 1.0, None, ALU.add)
            dve.wait(m, msg)
            for b in range(GB):
                m = dve.do(V.max, top[:, b, :], PR[:, b, :])
            yield
            dve.wait(m)
            for b in range(GB):
                m = dve.do(V.match_replace, MR[:, b, :], top[:, b, :], PR[:, b, :], 0.0)
            dve.wait(m)
            m = dve.do(V.tensor_tensor, rest[:, :, 0:E], PR[:, :, TOPK:], MR[:, :, TOPK:], ALU.subtract)
            msg = dve.do(V.reciprocal, C[:, :, E], sg)
            yield
            dve.wait(m)
            m = dve.do(V.tensor_reduce, s4, rest[:, :, 0:E], AX.X, ALU.add)
            dve.wait(m)
            m = dve.do(V.tensor_scalar, s4, s4, 1e-9, None, ALU.max)
            yield
            dve.wait(m)
            m = dve.do(V.reciprocal, r4, s4)
            dve.wait(m)
            m = dve.do(V.tensor_tensor, C[:, :, 0:E], rest[:, :, 0:E],
                       r4.unsqueeze(2).broadcast_to([P, GB, E]), ALU.mult)
            yield
            dve.wait(m, msg)
            src = C
            for part in range(NSPLIT):
                piece = CS[:, :, part * CW:(part + 1) * CW]
                m = dve.do(V.tensor_copy, piece, src)
                dve.wait(m)
                if part < NSPLIT - 1:
                    m = dve.do(V.tensor_tensor, rest, src, piece, ALU.subtract)
                    dve.wait(m)
                    src = rest
            yield
            yield
            cb = side_work.next_bank()
            pe.wait(m, got_idb, cb.free)
            bb = cb.t[:, :].bitcast(BF16)
            for b in range(GB):
                m = pe.do(T.transpose, bb[0:NSPLIT * CW, b * P:(b + 1) * P], CS[:, b, 0:NSPLIT * CW],
                          identb[:, :])
            yield
            dve.wait(m)
            cb.free = m = dve.do(V.tensor_copy, combT[0:NSPLIT * CW, ts], bb[0:NSPLIT * CW, 0:GT])
            comb_ready[g] = m
            yield

        def experts(scope):
            scope_far = scope.enter_context(ExitStack())
            WKV_UNITS = 46
            LAG = 2
            UW, DW = 2 * KT * P, D
            NU, ND = 3, 3 + LAG
            raw4 = columns(kept, "narrow_attention_weights", KT * 3 * D).take(KT * 3 * D).rearrange(
                "p (k c) -> p k c", k=KT)
            NEAR = NJ - FAR_COLUMNS // JW
            wr = columns(scope, "experts_split", 2 * (NU * UW + ND * DW + 3 * GT), F32R)
            ar = columns(scope, "experts", SBUF_COLUMNS - FAR_COLUMNS - KT * 3 * D - wr.width)
            near = ar.take(NEAR * JW).rearrange("p (j c) -> p j c", j=NEAR)
            sel = ar.take(NJ * P // 2).bitcast(BF16)
            gate = [ar.take(GT) for _ in range(2)]
            hid = [ar.take(GT) for _ in range(2)]
            sm.at = small_base
            up_slot = [[wr.take(UW) for _ in range(2)] for _ in range(NU)]
            down_slot = [[wr.take(DW) for _ in range(2)] for _ in range(ND)]
            hsplit = [[wr.take(GT) for _ in range(2)] for _ in range(3)]
            raw, got_w = {}, {}

            def load_tiles(tiles, first, counts):
                j = 0
                for count in counts:
                    m = load(f"load_moe{first + j}", tiles[:, j:j + count, :],
                             io["moe"][:, first + j:first + j + count, :])
                    for i in range(j, j + count):
                        raw[first + i], got_w[first + i] = tiles[:, i, :], m
                    j += count

            load_tiles(near, 0, (1, 1))
            got_sel = load("load_sel", sel, io["sel"])
            load_tiles(near[:, 2:, :], 2, (2, 4, 4, 4))
            got_w4 = load("load_w4", raw4, io["wqkv1"])
            acc = banks[0:2]
            ring = banks[2:8]
            nring = [0]

            def next_bank():
                nring[0] += 1
                return ring[(nring[0] - 1) % 6]

            up_free, down_free = [None] * NU, [None] * ND
            up_ready, down_ready = {}, {}
            h_ready = {}
            hs_free = [None] * 3
            gate_free, hid_free = [None] * 2, [None] * 2
            runs = [(g, 0, NEAR) for g in range(3)] + [(g, NEAR, NJ) for g in range(3)] + [(3, 0, NJ)]
            steps = [(g, j, j == first, j == end - 1) for g, first, end in runs for j in range(first, end)]

            def split_weights(n):
                g, j, first, last = steps[n]
                s, d = up_slot[n % NU], down_slot[n % ND]
                up_ready[n] = split(s[0], s[1], raw[j][:, 0:UW], [got_w[j], up_free[n % NU]],
                                    dve, V.tensor_copy, pool, G.tensor_tensor)
                down_ready[n] = split(d[0], d[1], raw[j][:, UW:], [got_w[j], down_free[n % ND]],
                                      dve, V.tensor_copy, pool, G.tensor_tensor)

            def up(n):
                g, j, first, last = steps[n]
                u, v = n % 2, n % 3
                hi, lo = (part.rearrange("p (m c) -> p m c", m=2 * KT) for part in up_slot[n % NU])
                ts = slice(g * GT, (g + 1) * GT)
                pe.wait(up_ready[n], comb_ready[g])
                got = []
                for m in range(2):
                    bank = next_bank()
                    done = project(bank, [(hi[:, 2 * m + k, :], lo[:, 2 * m + k, :], XT[:, 0, k, ts], XT[:, 1, k, ts])
                                          for k in range(KT)])
                    got.append((bank, done))
                up_free[n % NU] = done
                bank = next_bank()
                pe.wait(bank.free, got_sel)
                done = pe.do(T.matmul, bank.t[:, :], sel[:, j * P:(j + 1) * P], combT[:, ts], start=True, stop=True)
                (gb, gd), (ub, ud), (cb, cd) = got[0], got[1], (bank, done)
                act.wait(gd, gate_free[u])
                gb.free = m = act.do(S.activation, gate[u], gb.t[:, :], ACT.Silu)
                dve.wait(m, ud, hid_free[u])
                gate_free[u] = ub.free = m = dve.do(V.tensor_tensor, hid[u], gate[u], ub.t[:, :], ALU.mult)
                dve.wait(m, cd)
                cb.free = m = dve.do(V.tensor_tensor, hid[u], hid[u], cb.t[:, :], ALU.mult)
                h_ready[n] = hid_free[u] = split(hsplit[v][0], hsplit[v][1], hid[u], [m, hs_free[v]],
                                                 act, S.copy, pool, G.tensor_tensor)

            def down(n):
                g, j, first, last = steps[n]
                v = n % 3
                hi, lo = down_slot[n % ND]
                pe.wait(h_ready[n], down_ready[n])
                for d in range(KT):
                    if first:
                        pe.wait(acc[d].free)
                    cs = slice(d * P, (d + 1) * P)
                    pe.quiet(T.matmul, acc[d].t[:, :], hi[:, cs], hsplit[v][0], start=first, stop=False)
                    pe.quiet(T.matmul, acc[d].t[:, :], hi[:, cs], hsplit[v][1], start=False, stop=False)
                    m = pe.do(T.matmul, acc[d].t[:, :], lo[:, cs], hsplit[v][0], start=False, stop=last)
                down_free[n % ND] = hs_free[v] = m
                if last:
                    for d in range(KT):
                        act.wait(m, gate_free[d], hid_free[d])
                        acc[d].free = r = act.do(S.copy, gate[d], acc[d].t[:, :])
                        bank = next_bank()
                        pe.wait(r, bank.free)
                        for b in range(GB):
                            r = pe.do(T.transpose, bank.t[:, b * P:(b + 1) * P], gate[d][:, b * P:(b + 1) * P],
                                      ident[:, :])
                        gate_free[d] = r
                        dve.wait(r)
                        bank.free = x_ready[g] = dve.do(
                            V.tensor_tensor, X[:, g * GB:(g + 1) * GB, d * P:(d + 1) * P],
                            bank.t[:, :].rearrange("p (b t) -> p b t", b=GB),
                            X[:, g * GB:(g + 1) * GB, d * P:(d + 1) * P], ALU.add)

            side_work.next_bank = next_bank
            side_work.add(routing(1), wkv.group(2), routing(2), wkv.group(3))
            n = len(steps)
            split_weights(0)
            split_weights(1)
            for i in range(n + LAG):
                if i == WKV_UNITS:
                    side_work.finish()
                    side_work.add(routing(3))
                    dve.wait(got_w4, got_vec)
                    for k in range(KT):
                        for cs, gain in ((slice(0, D), 36 + k), (slice(D, 3 * D), 38 + k)):
                            m = dve.do(V.tensor_scalar, raw4[:, k, cs], raw4[:, k, cs], vec[:, gain:gain + 1], None,
                                       ALU.mult)
                    next_weights[:] = [raw4, m]
                    right.close()
                    sp.wait(pe.mark, dve.mark, act.mark, pool.mark)
                    far = columns(scope_far, "experts_far", FAR_COLUMNS, F32, "right")
                    load_tiles(far.take(FAR_COLUMNS).rearrange("p (j c) -> p j c", j=NJ - NEAR), NEAR, (1, 3, 4, 4))
                if i + 2 < n:
                    split_weights(i + 2)
                if i < n:
                    while steps[i][0] not in comb_ready:
                        side_work.step()
                    up(i)
                side_work.step(2 if i < WKV_UNITS else 1)
                if i >= LAG:
                    down(i - LAG)
                    g, j, first, last = steps[i - LAG]
                    if last and j == NJ - 1 and g < NG - 1:
                        side_work.add(second_norm(g))
                side_work.step()
            side_work.finish()
            phase_end()

        class Context:

            def open(self):
                self.raw = columns(right, "context_weights", KT * 2 * 512, F32, "right").take(KT * 2 * 512)
                self.scope = ExitStack()
                w = columns(self.scope, "context_weights_split", 2 * KT * 2 * 512, F32R, "right")
                ar = columns(self.scope, "context", FAR_COLUMNS - 3 * KT * 2 * 512, F32, "right")
                self.hi, self.lo = (w.take(KT * 2 * 512).rearrange("p (k c) -> p k c", k=KT) for _ in range(2))
                raw = self.raw.rearrange("p (k c) -> p k c", k=KT)
                self.bias = ar.take(2 * 512)
                self.stage = [ar.take(KT * GT).rearrange("p (k t) -> p k t", k=KT) for _ in range(2)]
                got_w = load("load_wkv5", raw, io["wkvx"])
                self.got_bias = load("load_bias5", self.bias, io["bkvx"].partition_broadcast(P))
                self.loaded = [load(f"load_ctx5_{g}", self.stage[g], io["ctxT"][:, :, g * GT:(g + 1) * GT])
                               for g in range(2)]
                side_work.add(self.parts(raw, got_w))

            def parts(self, raw, got_w):
                for k in range(KT):
                    for c in range(0, 2 * 512, 256):
                        cs = slice(c, c + 256)
                        self.w_ready = split(self.hi[:, k, cs], self.lo[:, k, cs], raw[:, k, cs], [got_w],
                                             pool, G.tensor_copy, pool, G.tensor_tensor)
                        yield

        context = Context()

        def narrow_attention(scope):
            wr = columns(scope, "narrow_attention_split", 2 * KT * 3 * D, F32R)
            ar = columns(scope, "narrow_attention", SBUF_COLUMNS - FAR_COLUMNS - 3 * KT * 3 * D)
            w_hi, w_lo = (wr.take(KT * 3 * D).rearrange("p (k c) -> p k c", k=KT) for _ in range(2))
            wo = ar.take(KT * D).rearrange("p (k c) -> p k c", k=KT)
            bias, bo = ar.take(3 * D), ar.take(D)
            mask8 = ar.take(8)
            xn = tiles_xn
            qk = [ar.take(2 * D) for _ in range(GB)]
            vv = [ar.take(D) for _ in range(2 * GB)]
            qsq = ar.take(2 * D)
            qT = [ar.take(2 * P).rearrange("p (i t) -> p i t", i=2) for _ in range(2 * GB)]
            kT = [ar.take(2 * P).rearrange("p (i t) -> p i t", i=2) for _ in range(2 * GB)]
            kbd = [ar.take(2 * 8 * P).rearrange("p (i h t) -> p i h t", i=2, h=8) for _ in range(2)]
            Pm = [ar.take(512).rearrange("p (h k) -> p h k", h=HG) for _ in range(3)]
            PT = [ar.take(512).rearrange("p (h k) -> p h k", h=HG) for _ in range(2)]
            z = [ar.take(D) for _ in range(2)]
            zT = [ar.take(2 * P).rearrange("p (i t) -> p i t", i=2) for _ in range(2)]
            sm.at = small_base
            qss = ar.take(2 * GB * 32).rearrange("p (s b c) -> p s b c", s=2, b=GB)
            gg = sm.take(2)
            negmax = [sm.take(HG) for _ in range(3)]
            rowsum = [sm.take(H) for _ in range(2)]
            rinv = [sm.take(H) for _ in range(2)]

            got_wo = load("load_wo4", wo, io["wo1"])
            got_bias = load("load_bias4", bias, io["bqkv1"].partition_broadcast(P))
            got_bo = load("load_bo4", bo, io["bo1"].partition_broadcast(P))
            got_mask8 = load("load_mask8", mask8, io["mask8"])
            w_ready = [split(w_hi[:, k], w_lo[:, k], next_weights[0][:, k], [next_weights[1]],
                             act, S.copy, dve, V.tensor_tensor) for k in range(KT)]
            m = dve.do(V.tensor_tensor, gg[:, 0:1], vec[:, 40:41], vec[:, 40:41], ALU.mult)
            dve.wait(m)
            context.open()
            gg_ready = dve.do(V.tensor_scalar, gg[:, 0:1], gg[:, 0:1], float(DS) ** -0.5, None, ALU.mult)

            fb, sbank, tbank, zbank, obank = banks[0:2], banks[2:4], banks[4:6], banks[6], banks[7]
            xt_ready, bo_added = second_xt, {}
            qk_ready, v_ready, head_ready, kt_ready, kbd_ready = {}, {}, {}, {}, {}
            v_free, kt_free, qt_free = [None] * 8, [None] * 8, [None] * 8
            head_normed = {}
            qk_free, kbd_free = [None] * GB, [None] * 2
            qsq_free = [None]

            tiles = second_tiles

            def prep_moments(g):
                moments(g, then_rms=True)

            def prep_norm(g):
                tiles[g] = normalised(g, xn)

            def prep_channels(g, kt):
                xt_ready[g] = split_channels(g, xn, tiles[g], kt, fb[kt])

            def prep_bias(g):
                dve.wait(got_bo, tiles[g][-1])
                for b in range(GB):
                    m = dve.do(V.tensor_tensor, X[:, g * GB + b, :], X[:, g * GB + b, :], bo, ALU.add)
                bo_added[g] = m

            def prep_project(g, b):
                bb = g * GB + b
                ts = slice(bb * P, (bb + 1) * P)
                pe.wait(xt_ready[g], *w_ready)
                done = project(fb[0], [(XT[:, 0, k, ts], XT[:, 1, k, ts], w_hi[:, k, 0:512], w_lo[:, k, 0:512])
                                       for k in range(KT)])
                dve.wait(done, got_bias, qk_free[b])
                m = fb[0].free = dve.do(V.tensor_tensor, qk[b], fb[0].t[:, :], bias[:, 0:512], ALU.add)
                done = project(fb[1], [(XT[:, 0, k, ts], XT[:, 1, k, ts], w_hi[:, k, 512:], w_lo[:, k, 512:])
                                       for k in range(KT)])
                dve.wait(done, v_free[bb % 8])
                v_ready[bb] = fb[1].free = dve.do(V.tensor_tensor, vv[bb % 8], fb[1].t[:, 0:D], bias[:, 512:],
                                                  ALU.add)
                pool.wait(m, qsq_free[0])
                m = pool.do(G.tensor_tensor, qsq, qk[b], qk[b], ALU.mult)
                dve.wait(m)
                qsq_free[0] = qk_ready[bb] = dve.do(V.tensor_reduce, qss[:, g % 2, b, :],
                                                    qsq.rearrange("p (c d) -> p c d", d=DS), AX.X, ALU.add)

            def prep_scale(g):
                s = g % 2
                act.wait(qk_ready[g * GB + GB - 1])
                head_ready[g] = act.do(S.activation, qss[:, s], qss[:, s], ACT.Sqrt, bias=eps_rms[:, 0:1],
                                       scale=1.0 / DS)

            def prep_head_norm(g):
                s = g % 2
                dve.wait(head_ready[g])
                pool.wait(dve.do(V.reciprocal, qss[:, s], qss[:, s]))
                for b in range(GB):
                    r3 = qk[b].rearrange("p (c d) -> p c d", d=DS)
                    head_normed[g * GB + b] = pool.do(
                        G.tensor_tensor, r3, r3, qss[:, s, b, :].unsqueeze(2).broadcast_to([P, 32, DS]), ALU.mult)

            def prep_heads(g, b):
                bb, bank = g * GB + b, fb[b % 2]
                pe.wait(head_normed[bb], bank.free)
                for i in range(4):
                    m = pe.do(T.transpose, bank.t[:, i * P:(i + 1) * P], qk[b][:, i * P:(i + 1) * P], ident[:, :])
                qk_free[b] = m
                act.wait(m, qt_free[bb % 8], kt_free[bb % 8], gg_ready)
                act.do(S.activation, qT[bb % 8], bank.t[:, 0:256].rearrange("p (i t) -> p i t", i=2),
                       ACT.Identity, scale=gg[:, 0:1])
                kt_ready[bb] = bank.free = act.do(S.copy, kT[bb % 8],
                                                   bank.t[:, 256:512].rearrange("p (i t) -> p i t", i=2))

            def spread_keys(bb):
                s = bb % 2
                pool.wait(kt_ready[bb], kbd_free[s], got_mask8)
                for i in range(2):
                    m = pool.do(G.tensor_tensor, kbd[s][:, i], kT[bb % 8][:, i].unsqueeze(1).broadcast_to([P, 8, P]),
                                mask8.unsqueeze(2).broadcast_to([P, 8, P]), ALU.mult)
                kt_free[bb % 8] = kbd_ready[bb] = m

            probs_ready, exp_ready, pt_ready = {}, {}, {}
            P_free, PT_free, z_free, zT_free = [None] * 3, [None] * 2, [None] * 2, [None] * 2

            def scores(n):
                bb, q4 = divmod(n, 4)
                u, v, s = n % 2, n % 3, bb % 2
                bank = sbank[u]
                pe.wait(bank.free, kbd_ready[bb])
                m = pe.do(T.matmul, bank.t[:, :], qT[bb % 8][:, q4 // 2, :],
                          kbd[s][:, q4 // 2, (q4 % 2) * 4:(q4 % 2) * 4 + 4, :].rearrange("p h t -> p (h t)"),
                          start=True, stop=True)
                kbd_free[s] = qt_free[bb % 8] = m
                s4 = bank.t[:, :].rearrange("p (h k) -> p h k", h=HG)
                dve.wait(m)
                m = dve.do(V.tensor_reduce, negmax[v], s4, AX.X, ALU.max, negate=True)
                act.wait(m, P_free[v])
                for h in range(HG):
                    m = act.do(S.activation, Pm[v][:, h, :], s4[:, h, :], ACT.Exp, bias=negmax[v][:, h:h + 1],
                               accum_out=rowsum[s][:, q4 * 4 + h:q4 * 4 + h + 1])
                bank.free = exp_ready[n] = m

            def transposes(n):
                u, v = n % 2, n % 3
                bank = tbank[u]
                pe.wait(bank.free, exp_ready[n])
                for h in range(HG):
                    m = pe.do(T.transpose, bank.t[:, h * P:(h + 1) * P], Pm[v][:, h, :], ident[:, :])
                P_free[v] = m
                dve.wait(m, PT_free[u])
                pt_ready[n] = bank.free = dve.do(V.tensor_copy, PT[u], bank.t[:, :].rearrange(
                    "p (h k) -> p h k", h=HG))

            def values(n):
                bb, q4 = divmod(n, 4)
                u, s = n % 2, bb % 2
                pe.wait(pt_ready[n], v_ready[bb])
                if q4 == 0:
                    pe.wait(zbank.free)
                for h in range(HG):
                    hh = q4 * HG + h
                    m = pe.do(T.matmul, zbank.t[:, hh * DS:(hh + 1) * DS], PT[u][:, h, :],
                              vv[bb % 8][:, hh * DS:(hh + 1) * DS], start=True, stop=True)
                PT_free[u] = m
                if q4 == 3:
                    v_free[bb % 8] = m
                    dve.wait(exp_ready[n])
                    r = dve.do(V.reciprocal, rinv[s], rowsum[s])
                    dve.wait(m, r, z_free[s])
                    z_done[bb] = zbank.free = dve.do(
                        V.tensor_tensor, z[s].rearrange("p (h d) -> p h d", h=H),
                        zbank.t[:, 0:D].rearrange("p (h d) -> p h d", h=H),
                        rinv[s].unsqueeze(2).broadcast_to([P, H, DS]), ALU.mult)

            z_done = {}

            zt_ready = {}

            def turn(bb):
                s = bb % 2
                pe.wait(z_done[bb], obank.free)
                for i in range(2):
                    m = pe.do(T.transpose, obank.t[:, i * P:(i + 1) * P], z[s][:, i * P:(i + 1) * P], ident[:, :])
                z_free[s] = m
                act.wait(m, zT_free[s])
                zt_ready[bb] = act.do(S.copy, zT[s], obank.t[:, 0:256].rearrange("p (i t) -> p i t", i=2))

            def output(bb):
                s, g = bb % 2, bb // GB
                pe.wait(zt_ready[bb], got_wo)
                for i in range(2):
                    m = pe.do(T.matmul, obank.t[:, 256:512], zT[s][:, i, :], wo[:, i, :], start=i == 0, stop=i == 1)
                zT_free[s] = m
                dve.wait(m, bo_added[g], x_ready[g])
                x_ready[g] = obank.free = dve.do(V.tensor_tensor, X[:, bb, :], obank.t[:, 256:512], X[:, bb, :],
                                                 ALU.add)

            def preparation(g):
                return {0: [(prep_moments, g)], 1: [(prep_norm, g)],
                        2: [(prep_channels, g, 0), (prep_channels, g, 1)],
                        3: [(prep_project, g, 0)], 4: [(prep_project, g, 1)], 6: [(prep_project, g, 2)],
                        7: [(prep_project, g, 3)], 8: [(prep_scale, g), (prep_bias, g)], 9: [(prep_head_norm, g)],
                        11: [(prep_heads, g, 0)], 12: [(prep_heads, g, 1)], 13: [(prep_heads, g, 2)],
                        14: [(prep_heads, g, 3)]}

            for at, work in sorted(preparation(0).items()):
                for fn, *args in work:
                    if fn not in (prep_moments, prep_norm, prep_channels):
                        fn(*args)
            spread_keys(0)
            steps = B * 4
            for n in range(steps + 5):
                g, u = divmod(n, 16)
                if n < steps:
                    if n % 4 == 0 and n // 4 + 1 < B:
                        spread_keys(n // 4 + 1)
                    scores(n)
                if g + 1 < NG and n < steps:
                    for fn, *args in preparation(g + 1).get(u, []):
                        if g + 1 == NG - 1 or fn not in (prep_moments, prep_norm, prep_channels):
                            fn(*args)
                if 2 <= n <= steps + 1:
                    transposes(n - 2)
                if 3 <= n <= steps + 2:
                    values(n - 3)
                if n >= 24 and n % 4 == 1:
                    side_work.step()
                if n >= 7 and (n - 7) % 4 == 0:
                    turn((n - 7) // 4)
                if n >= 8 and (n - 8) % 4 == 0:
                    output((n - 8) // 4)
            phase_end()

        def cross_attention(scope):
            wr = columns(scope, "query_weights_split", 2 * 2 * KT * 512, F32R)
            wq = [[wr.take(KT * 512).rearrange("p (k c) -> p k c", k=KT) for _ in range(2)] for _ in range(2)]
            near = SBUF_COLUMNS + KEPT_COLUMNS - FAR_COLUMNS - wr.width
            cross = 2 * B * 512 + KT * 512 + 2 * HG * D
            ar = columns(scope, "cross_attention", cross)
            kT = ar.take(B * NKV * P).rearrange("p (b h t) -> p b h t", b=B, h=NKV)
            vv = ar.take(B * NKV * DH).rearrange("p (b c) -> p b c", b=B)
            raw = ar.take(KT * 512).rearrange("p (k c) -> p k c", k=KT)
            wo = [ar.take(HG * D).rearrange("p (h d) -> p h d", h=HG) for _ in range(2)]
            sm.at = small_base
            kscale = sm.take(2)
            kss = sm.take(2 * GB * NKV).rearrange("p (s b c) -> p s b c", s=2, b=GB)

            weights_ready, wo_ready = {}, {}
            raw_free, wr_free, wo_free = [None], [None] * 2, [None] * 2

            def fetch_weights(hg):
                s = hg % 2
                sp.wait(raw_free[0], wo_free[s])
                got = load(f"load_wq5_{hg}", raw, io["wqx"][:, hg])
                wo_ready[hg] = load(f"load_wo5_{hg}", wo[s], io["wox"][:, hg])
                raw_free[0] = weights_ready[hg] = split(wq[s][0], wq[s][1], raw, [got, wr_free[s]],
                                                        pool, G.tensor_copy, pool, G.tensor_tensor)

            first = ExitStack()
            ar = columns(first, "context_keys", near - cross)
            key = [ar.take(512) for _ in range(GB)] + [context.raw[:, b * 512:(b + 1) * 512] for b in range(GB)]
            ksq = ar.take(512)
            kv_hi, kv_lo, bias, stage = context.hi, context.lo, context.bias, context.stage
            got_bias, w_ready = context.got_bias, context.w_ready
            dve.wait(got_vec)
            m = dve.do(V.tensor_tensor, kscale[:, 0:1], vec[:, 57:58], vec[:, 58:59], ALU.mult)
            dve.wait(m)
            kscale_ready = dve.do(V.tensor_scalar, kscale[:, 0:1], kscale[:, 0:1],
                                  1.0 / float(np.sqrt(np.float32(DH))), None, ALU.mult)
            stage_free = [None] * 2
            ct_ready = []
            for g in range(NG):
                ts = slice(g * GT, (g + 1) * GT)
                if g < 2:
                    got = context.loaded[g]
                else:
                    sp.wait(stage_free[g % 2])
                    got = load(f"load_ctx5_{g}", stage[g % 2], io["ctxT"][:, :, ts])
                stage_free[g % 2] = m = split(XT[:, 0, :, ts], XT[:, 1, :, ts], stage[g % 2], [got],
                                              act, S.copy, dve, V.tensor_tensor)
                ct_ready.append(m)
            key_free = [None] * 8
            ksq_free = None
            ring, at = banks[0:6], 0

            def heads_out(g):
                s = g % 2
                act.wait(kss_ready[g])
                m = act.do(S.activation, kss[:, s], kss[:, s], ACT.Sqrt, bias=eps_qk[:, 0:1], scale=1.0 / DH)
                yield
                dve.wait(m)
                r = dve.do(V.reciprocal, kss[:, s], kss[:, s])
                normed = []
                for b in range(GB):
                    k3 = key[(g * GB + b) % 8].rearrange("p (h d) -> p h d", h=NKV)
                    pool.wait(r)
                    normed.append(pool.do(G.tensor_tensor, k3, k3,
                                          kss[:, s, b, :].unsqueeze(2).broadcast_to([P, NKV, DH]), ALU.mult))
                for b in range(GB):
                    yield
                    kb = key[(g * GB + b) % 8]
                    bank = banks[7]
                    pe.wait(normed[b], bank.free)
                    for h in range(NKV):
                        m = pe.do(T.transpose, bank.t[:, h * P:(h + 1) * P], kb[:, h * P:(h + 1) * P], ident[:, :])
                    key_free[(g * GB + b) % 8] = m
                    act.wait(m, kscale_ready)
                    bank.free = act.do(S.activation, kT[:, g * GB + b], bank.t[:, :].rearrange(
                        "p (h t) -> p h t", h=NKV), ACT.Identity, scale=kscale[:, 0:1])
                yield

            xt_ready = {}
            kss_ready = {}
            side_work.next_bank = lambda: banks[6]

            def layer_norm(g):
                moments(g)
                yield
                marks = normalised(g, tiles_xn)
                yield
                yield
                for kt in range(KT):
                    xt_ready[g] = split_channels(g, tiles_xn, marks, kt, side_work.next_bank())
                    yield

            for g in range(NG):
                for b in range(GB):
                    side_work.step()
                    bb = g * GB + b
                    ts = slice(bb * P, (bb + 1) * P)
                    pe.wait(ct_ready[g], w_ready)
                    kbank, vbank = ring[at % 6], ring[(at + 1) % 6]
                    at += 2
                    done = project(kbank, [(XT[:, 0, k, ts], XT[:, 1, k, ts], kv_hi[:, k, 0:512], kv_lo[:, k, 0:512])
                                           for k in range(KT)])
                    dve.wait(done, got_bias, key_free[bb % 8])
                    m = kbank.free = dve.do(V.tensor_tensor, key[bb % 8], kbank.t[:, :], bias[:, 0:512], ALU.add)
                    side_work.step()
                    done = project(vbank, [(XT[:, 0, k, ts], XT[:, 1, k, ts], kv_hi[:, k, 512:], kv_lo[:, k, 512:])
                                           for k in range(KT)])
                    dve.wait(done)
                    vbank.free = dve.do(V.tensor_tensor, vv[:, bb, :], vbank.t[:, :], bias[:, 512:], ALU.add)
                    side_work.step()
                    act.wait(m, ksq_free)
                    m = act.do(S.activation, ksq, key[bb % 8], ACT.Square)
                    dve.wait(m)
                    ksq_free = dve.do(V.tensor_reduce, kss[:, g % 2, b, :],
                                      ksq.rearrange("p (h d) -> p h d", h=NKV), AX.X, ALU.add)
                kss_ready[g] = ksq_free
                if g == NG - 1:
                    side_work.finish()
                side_work.add(layer_norm(g), heads_out(g))
                if g == 0:
                    fetch_weights(0)
            phase_end()
            first.close()
            context.scope.close()

            ar = columns(scope, "cross_attention_heads", 2 * HG * GT + 2 * GT + 4 * 2 * 512 + P)
            qT = [ar.take(HG * GT).rearrange("p (h t) -> p h t", h=HG) for _ in range(2)]
            qsq = [ar.take(GT) for _ in range(2)]
            Smask, Pm, PT, ZT = ([four(ar.take(512)) for _ in range(2)] for _ in range(4))
            mask = ar.take(P)
            negmax = [sm.take(HG) for _ in range(2)]
            sums = [sm.take(HG) for _ in range(2)]
            rinv = [sm.take(HG) for _ in range(2)]
            rq = [sm.take(GB * HG) for _ in range(2)]
            ones = sm.take(2)
            ones_ready = dve.do(V.memset, ones, 1.0)
            got_mask = load("load_mask5", mask, io["mask"])

            sbank, tbank, qbank, zbank, obank = banks[2:4], banks[4], banks[5], banks[6], banks[7]
            nfill = [0]
            q_ready, rq_ready = {}, {}
            q_free, q_squared, rq_free, qsq_free = [None] * 2, [None] * 2, [None] * 2, [None] * 2
            qsq_ready = {}

            def fill_bank():
                nfill[0] += 1
                return banks[(nfill[0] - 1) % 2]

            side_work.next_bank = fill_bank

            def fill(grp, h):
                hg, g = divmod(grp, NG)
                s, hh = grp % 2, hg * HG + h
                bank = fill_bank()
                cs, ts = slice(h * DH, (h + 1) * DH), slice(g * GT, (g + 1) * GT)
                hi, lo = wq[hg % 2]
                pe.wait(weights_ready[hg], xt_ready[g])
                done = project(bank, [(hi[:, k, cs], lo[:, k, cs], XT[:, 0, k, ts], XT[:, 1, k, ts])
                                      for k in range(KT)])
                wr_free[hg % 2] = done
                act.wait(done, q_free[s], q_squared[s])
                m = bank.free = q_ready[grp] = act.do(S.activation, qT[s][:, h, :], bank.t[:, :], ACT.Identity,
                                                      bias=vec[:, 41 + hh:42 + hh])
                pool.wait(m, qsq_free[h % 2])
                q_squared[s] = qsq_ready[grp, h] = pool.do(G.tensor_tensor, qsq[h % 2], qT[s][:, h, :],
                                                           qT[s][:, h, :], ALU.mult)

            def sum_squares(grp, h):
                s = grp % 2
                pe.wait(qsq_ready[grp, h], qbank.free, ones_ready)
                for b in range(GB):
                    c = b * HG + h
                    m = pe.do(T.matmul, qbank.t[:, c:c + 1], qsq[h % 2][:, b * P:(b + 1) * P], ones[:, 0:1],
                              start=True, stop=True)
                qsq_free[h % 2] = m
                if h == HG - 1:
                    act.wait(m, rq_free[s])
                    m = qbank.free = act.do(S.activation, rq[s], qbank.t[:, 0:GB * HG], ACT.Sqrt,
                                            bias=eps_qk[:, 0:1], scale=1.0 / DH)
                    dve.wait(m)
                    rq_ready[grp] = dve.do(V.reciprocal, rq[s], rq[s])

            max_ready, exp_ready, probs_ready, pt_ready, z_ready = {}, {}, {}, {}, {}
            Sm_free, P_free, PT_free, ZT_free = [None] * 2, [None] * 2, [None] * 2, [None] * 2

            def scores(n):
                grp, b = divmod(n, GB)
                hg, g = divmod(grp, NG)
                s, u = grp % 2, n % 2
                bank = sbank[u]
                pe.wait(bank.free, q_ready[grp])
                ts = slice(b * P, (b + 1) * P)
                for h in range(HG):
                    m = pe.do(T.matmul, bank.t[:, h * P:(h + 1) * P], qT[s][:, h, ts], kT[:, g * GB + b, hg, :],
                              start=True, stop=True)
                q_free[s] = m
                dve.wait(m, Sm_free[u], rq_ready[grp], got_mask)
                for h in range(HG):
                    c = b * HG + h
                    m = dve.do(V.scalar_tensor_tensor, out=Smask[u][:, h, :], in0=bank.t[:, h * P:(h + 1) * P],
                               scalar=rq[s][:, c:c + 1], in1=mask, op0=ALU.mult, op1=ALU.add)
                bank.free = rq_free[s] = m
                max_ready[n] = row_max(negmax[u], Smask[u], m)

            def exps(n):
                u = n % 2
                exp_ready[n] = Sm_free[u] = exponentials(Pm[u], Smask[u], negmax[u], sums[u], max_ready[n],
                                                         P_free[u])

            def norm(n):
                u = n % 2
                probs_ready[n] = normalise(Pm[u], sums[u], rinv[u], exp_ready[n])

            def transposes(n):
                u, bank = n % 2, tbank
                pe.wait(bank.free, probs_ready[n])
                for h in range(HG):
                    m = pe.do(T.transpose, bank.t[:, h * P:(h + 1) * P], Pm[u][:, h, :], ident[:, :])
                P_free[u] = m
                act.wait(m, PT_free[u])
                pt_ready[n] = bank.free = act.do(S.copy, PT[u], four(bank.t[:, :]))

            def values(n):
                grp, b = divmod(n, GB)
                hg, g = divmod(grp, NG)
                u = n % 2
                pe.wait(zbank.free, pt_ready[n])
                m = pe.do(T.matmul, zbank.t[:, :], vv[:, g * GB + b, hg * DH:(hg + 1) * DH],
                          PT[u].rearrange("p h k -> p (h k)"), start=True, stop=True)
                PT_free[u] = m
                dve.wait(m, ZT_free[u])
                z_ready[n] = zbank.free = dve.do(V.tensor_copy, ZT[u], four(zbank.t[:, :]))

            def output(n):
                grp, b = divmod(n, GB)
                hg, g = divmod(grp, NG)
                u = n % 2
                pe.wait(obank.free, z_ready[n], wo_ready[hg])
                for h in range(HG):
                    m = pe.do(T.matmul, obank.t[:, 0:D], ZT[u][:, h, :], wo[hg % 2][:, h, :],
                              start=h == 0, stop=h == HG - 1)
                ZT_free[u] = m
                wo_free[hg % 2] = m
                dve.wait(m, x_ready[g])
                x_ready[g] = obank.free = dve.do(V.tensor_tensor, X[:, g * GB + b, :], obank.t[:, 0:D],
                                                 X[:, g * GB + b, :], ALU.add)

            for h in range(HG):
                fill(0, h)
                side_work.step(2)
                if h >= 1:
                    sum_squares(0, h - 1)
            fetch_weights(1)
            sum_squares(0, HG - 1)
            fill(1, 0)
            to_sum = (1, 0)
            nsteps = NHG * NG * GB
            for n in range(nsteps + 1):
                grp, b = divmod(n, GB)
                if n == 4:
                    side_work.finish()
                    right.close()
                    sp.wait(*key_free)
                    dve.wait(*key_free)
                    bitnet.open(SBUF_COLUMNS + KEPT_COLUMNS - wr.width - cross - ar.width)
                    side_work.add(bitnet.weights())
                ahead, h = divmod(n + GB + 1, GB)
                more = ahead < NHG * NG
                if n < nsteps:
                    scores(n)
                if n >= 1:
                    transposes(n - 1)
                if n < nsteps:
                    exps(n)
                if more:
                    fill(ahead, h)
                if n >= 1:
                    values(n - 1)
                if to_sum is not None:
                    sum_squares(*to_sum)
                to_sum = (ahead, h) if more else None
                if n < nsteps:
                    norm(n)
                side_work.step()
                if n >= 1:
                    output(n - 1)
                if n >= nsteps - GB * NG + GB and b == 0 and n < nsteps:
                    side_work.add(bitnet.quantise(grp % NG - 1))
                    side_work.step()
                elif n > nsteps - GB * NG + GB:
                    side_work.step()
                if b == 0 and grp % NG == 0 and 0 < grp // NG < NHG - 1:
                    fetch_weights(grp // NG + 1)
            phase_end()

        class BitNet:

            PIECES = [(i, i * BI, BI) for i in range(4)] + [(4 + i, 4 * BI + i * BJ * D // 2, BJ * D // 2)
                                                            for i in range(2)]

            def open(self, width):
                ar = columns(right, "bitnet_weights", width, F32, "right")
                self.width = width
                self.wq = ar.take((2 * KT * BI + BJ * D) // 2).bitcast(BF16)
                self.wgu = self.wq[:, 0:2 * KT * BI].rearrange("p (m k c) -> p m k c", m=2, k=KT)
                self.wdn = self.wq[:, 2 * KT * BI:].rearrange("p (j d) -> p j d", j=BJ)
                work = ar.at
                self.stage = [ar.take(BJ * D // 2) for _ in range(2)]
                self.ones = ar.take(P)
                ar.at = work
                self.xq = ar.take(GB * D // 2).bitcast(BF16)
                self.xqT = [ar.take(GB * D // 2).bitcast(BF16).rearrange("p (k t) -> p k t", k=KT)
                            for _ in range(NG - 1)]
                self.xq_free, self.xqT_ready, self.scales_ready = None, {}, {}

            def weights(self):
                free = [None] * 2
                count = [0]

                def fetch(name, at, n):
                    s = count[0] % 2
                    count[0] += 1
                    sp.wait(free[s])
                    src = io["bitgu"][:, at:at + n] if at < 4 * BI else io["bitdn"][:, at - 4 * BI:at - 4 * BI + n]
                    return s, self.stage[s][:, 0:n], load(name, self.stage[s][:, 0:n], src)

                m = dve.do(V.memset, self.ones, 1.0)
                for i, at, n in self.PIECES:
                    s, raw, got = fetch(f"load_magnitude{i}", at, n)
                    yield
                    dve.wait(got)
                    free[s] = m = dve.do(V.tensor_reduce, wsum[:, i:i + 1], raw, AX.X, ALU.add,
                                         apply_absolute_value=True)
                    yield
                bank = side_work.next_bank()
                pe.wait(m, bank.free)
                m = pe.do(T.matmul, bank.t[:, 0:6], self.ones, wsum[:, 0:6], start=True, stop=True)
                dve.wait(m)
                m = bank.free = dve.do(V.tensor_reduce, wmean[:, 0:3],
                                       bank.t[:, 0:6].rearrange("p (m i) -> p m i", i=2), AX.X, ALU.add)
                yield
                dve.wait(m)
                m = dve.do(V.tensor_scalar, wmean[:, 0:3], wmean[:, 0:3], 1.0 / (BI * D), 1e-5, ALU.mult, ALU.max)
                dve.wait(m)
                m = dve.do(V.reciprocal, wscale[:, 0:3], wmean[:, 0:3])
                yield
                dve.wait(m)
                for i, at, n in self.PIECES:
                    s, raw, got = fetch(f"load_ternary{i}", at, n)
                    yield
                    dve.wait(got)
                    m = dve.do(V.tensor_scalar, raw, raw, wscale[:, i // 2:i // 2 + 1], ROUND, ALU.mult, ALU.add)
                    yield
                    dve.wait(m)
                    m = dve.do(V.tensor_scalar, raw, raw, ROUND, 1.0, ALU.subtract, ALU.min)
                    dve.wait(m)
                    free[s] = self.wq_ready = dve.do(V.tensor_scalar, self.wq[:, at:at + n], raw, -1.0, None, ALU.max)
                    yield

            def quantise(self, g):
                s = g % 2
                xn, xq = tiles_xn[s], self.xq
                gs = slice(g * GB, (g + 1) * GB)
                moments(g)
                yield
                marks = normalised(g, tiles_xn)
                yield
                dve.wait(*marks)
                m = dve.do(V.tensor_reduce, step_x[:, gs], xn, AX.X, ALU.max, apply_absolute_value=True)
                yield
                dve.wait(m)
                m = dve.do(V.tensor_scalar, step_x[:, gs], step_x[:, gs], 1e-5, 1.0 / 127.0, ALU.max, ALU.mult)
                dve.wait(m)
                m = dve.do(V.reciprocal, per_x[:, gs], step_x[:, gs])
                dve.do(V.tensor_scalar, worth_gate[:, gs], step_x[:, gs], wmean[:, 0:1], None, ALU.mult)
                self.scales_ready[g] = dve.do(V.tensor_scalar, worth_up[:, gs], step_x[:, gs], wmean[:, 1:2], None,
                                              ALU.mult)
                dve.wait(m)
                for b in range(GB):
                    m = dve.do(V.tensor_scalar, xn[:, b, :], xn[:, b, :],
                               per_x[:, g * GB + b:g * GB + b + 1], ROUND, ALU.mult, ALU.add)
                yield
                dve.wait(m, self.xq_free)
                m = dve.do(V.tensor_scalar, xq, xn.rearrange("p b d -> p (b d)"), ROUND, None, ALU.subtract)
                for b in range(GB):
                    xn_free[s * GB + b] = m
                yield
                yield
                bank = side_work.next_bank()
                pe.wait(m, bank.free, got_idb)
                tv = bank.t[:, :].bitcast(BF16)
                for k in range(KT):
                    for b in range(GB):
                        m = pe.do(T.transpose, tv[:, k * GT + b * P:k * GT + (b + 1) * P],
                                  xq[:, b * D + k * P:b * D + (k + 1) * P], identb[:, :])
                self.xq_free = m
                act.wait(m)
                self.xqT_ready[g] = bank.free = act.do(S.copy, self.xqT[g], tv.rearrange("p (k t) -> p k t", k=KT))
                yield

        bitnet = BitNet()
        stores = []
        stored = signal("store_out")

        def store(g):
            sp.wait(x_ready[g])
            stores.append(sp.do(nc.sync.dma_start, out[:, g * GB:(g + 1) * GB, :], X[:, g * GB:(g + 1) * GB, :],
                                signal=stored, by=16))

        def bitnet_mlp(scope):
            ar = columns(scope, "bitnet", SBUF_COLUMNS + KEPT_COLUMNS - bitnet.width)
            wgu, wdn = bitnet.wgu, bitnet.wdn
            bitnet.xqT.append(ar.take(GB * D // 2).bitcast(BF16).rearrange("p (k t) -> p k t", k=KT))
            sg = [ar.take(BI) for _ in range(2)]
            hid = [ar.take(BI) for _ in range(3)]
            hq = [ar.take(BJ * P // 2).bitcast(BF16) for _ in range(3)]
            hT = [ar.take(BJ * P // 2).bitcast(BF16).rearrange("p (j t) -> p j t", j=BJ) for _ in range(2)]
            sm.at = small_base
            step_h, per_h, worth_down = sm.take(4), sm.take(4), sm.take(4)
            back = sm.take(2)
            dve.do(V.memset, back[:, 0:1], -ROUND)
            for s in range(3):
                cleared = dve.do(V.memset, hq[s][:, BI:], 0.0)
            hb, ob = banks[5:7], banks[7]
            side_work.next_bank = lambda: banks[4]

            sg_free, hid_free, hq_free, hT_free = [None] * 2, [None] * 3, [None] * 3, [None] * 2
            HB = BI // 2
            gated, summed, rounded, hq_ready, ht_ready = {}, {}, {}, {}, {}

            def up(bb):
                g, b = divmod(bb, GB)
                u, v = bb % 2, bb % 3
                pe.wait(bitnet.xqT_ready[g], bitnet.wq_ready)
                for i in range(4):
                    which, half = i % 2, i // 2
                    pe.wait(banks[i].free)
                    for k in range(KT):
                        m = pe.do(T.matmul, banks[i].t[:, 0:HB], bitnet.xqT[g][:, k, b * P:(b + 1) * P],
                                  wgu[:, which, k, half * HB:(half + 1) * HB], start=k == 0, stop=k == KT - 1)
                    if which == 0:
                        act.wait(m, bitnet.scales_ready[g], sg_free[u])
                        gate = banks[i].free = act.do(
                            S.activation, sg[u][:, half * HB:(half + 1) * HB], banks[i].t[:, 0:HB], ACT.Silu,
                            scale=worth_gate[:, bb:bb + 1])
                    else:
                        dve.wait(m, gate, hid_free[v])
                        m_h = banks[i].free = dve.do(
                            V.scalar_tensor_tensor, out=hid[v][:, half * HB:(half + 1) * HB],
                            in0=banks[i].t[:, 0:HB], scalar=worth_up[:, bb:bb + 1],
                            in1=sg[u][:, half * HB:(half + 1) * HB], op0=ALU.mult, op1=ALU.mult)
                sg_free[u] = m_h
                one = slice(v, v + 1)
                dve.wait(m_h)
                m = dve.do(V.tensor_reduce, step_h[:, one], hid[v], AX.X, ALU.max, apply_absolute_value=True)
                dve.wait(m)
                m = dve.do(V.tensor_scalar, step_h[:, one], step_h[:, one], 1e-5, 1.0 / 127.0, ALU.max, ALU.mult)
                dve.wait(m)
                m = dve.do(V.reciprocal, per_h[:, one], step_h[:, one])
                dve.do(V.tensor_scalar, worth_down[:, one], step_h[:, one], wmean[:, 2:3], None, ALU.mult)
                dve.wait(m)
                rounded[bb] = dve.do(V.tensor_scalar, hid[v], hid[v], per_h[:, one], ROUND, ALU.mult, ALU.add)

            def integers(bb):
                v = bb % 3
                act.wait(rounded[bb], hq_free[v], cleared)
                hq_ready[bb] = hid_free[v] = act.do(S.activation, hq[v][:, 0:BI], hid[v], ACT.Identity,
                                                    bias=back[:, 0:1])

            def turn(bb):
                u, v = bb % 2, bb % 3
                bank = hb[u]
                pe.wait(hq_ready[bb], bank.free)
                tv = bank.t[:, :].bitcast(BF16)
                for j in range(BJ):
                    m = pe.do(T.transpose, tv[:, j * P:(j + 1) * P], hq[v][:, j * P:(j + 1) * P], identb[:, :])
                hq_free[v] = m
                act.wait(m, hT_free[u])
                ht_ready[bb] = bank.free = act.do(S.copy, hT[u], tv[:, 0:BJ * P].rearrange("p (j t) -> p j t", j=BJ))

            def down(bb):
                g, b = divmod(bb, GB)
                u, v = bb % 2, bb % 3
                pe.wait(ht_ready[bb], ob.free)
                for j in range(BJ):
                    m = pe.do(T.matmul, ob.t[:, 0:D], hT[u][:, j, :], wdn[:, j, :], start=j == 0, stop=j == BJ - 1)
                hT_free[u] = m
                dve.wait(m, x_ready[g])
                x_ready[g] = ob.free = dve.do(V.scalar_tensor_tensor, out=X[:, bb, :], in0=ob.t[:, 0:D],
                                              scalar=worth_down[:, v:v + 1], in1=X[:, bb, :],
                                              op0=ALU.mult, op1=ALU.add)
                if b == GB - 1:
                    store(g)

            side_work.add(bitnet.quantise(NG - 1))
            for bb in range(B + 2):
                if bb < B:
                    while bb // GB not in bitnet.xqT_ready:
                        side_work.step()
                    up(bb)
                side_work.step()
                if 1 <= bb <= B:
                    integers(bb - 1)
                if 2 <= bb:
                    down(bb - 2)
                side_work.step()
                if 1 <= bb <= B:
                    turn(bb - 1)
                side_work.step()

        for n, phase in enumerate((self_attention, experts, narrow_attention, cross_attention, bitnet_mlp)):
            if n + 2 <= phases:
                with ExitStack() as scope:
                    phase(scope)
                if phase is narrow_attention:
                    kept.close()

        side_work.finish()
        kept.close()
        while len(stores) < NG:
            store(len(stores))
        sp.wait(stores[-1])

        block = ctx.enter_context(nc.Block())

        @block.sync
        def _(eng):
            sp.emit()

        @block.gpsimd
        def _(eng):
            pool.emit()

        @block.scalar
        def _(eng):
            act.emit()

        @block.vector
        def _(eng):
            dve.emit()

        @block.tensor
        def _(eng):
            pe.emit()


def layouts(x, ctx_2048, mask_1xSxS2_ff0, L0_attn_W_Q, L0_attn_W_K, L0_attn_W_V, L0_attn_W_O,
            L0_attn_b_Q, L0_attn_b_K, L0_attn_b_V, L0_attn_b_O, L0_xattn_time_decay, L0_xattn_time_first,
            L0_ffn_router_w, L0_ffn_w_gate, L0_ffn_w_up, L0_ffn_w_down, L0_ffn_sh_gate, L0_ffn_sh_up,
            L0_ffn_sh_down, L0_ffn_sh_gate_w, L1_attn_g_q, L1_attn_Wq, L1_attn_bq, L1_attn_g_kv,
            L1_attn_Wkv, L1_attn_bkv, L1_attn_g_head, L1_attn_Wo, L1_attn_bo, L1_xattn_Wq, L1_xattn_bq,
            L1_xattn_Wk, L1_xattn_bk, L1_xattn_Wv, L1_xattn_bv, L1_xattn_Wo, L1_xattn_qn_w,
            L1_xattn_kn_w, L1_ffn_w_gate, L1_ffn_w_up, L1_ffn_w_down):
    f = np.float32
    bf = mybir.dt.np(BF16)
    a = {}
    a["x"] = x.transpose(1, 0, 2)
    a["ctxT"] = ctx_2048.reshape(NT, KT, P).transpose(2, 1, 0)
    a["mask"] = mask_1xSxS2_ff0[0]
    a["ident"] = np.eye(P, dtype=f)
    a["identb"] = np.eye(P, dtype=f).astype(bf)
    a["causal"] = np.where(np.tril(np.ones((P, P), bool)), 0.0, NEG).astype(f)

    def columns(v):
        return v.reshape(-1, P).T
    vec = [L0_attn_b_Q.T, L0_attn_b_K.T, columns(L0_xattn_time_decay), columns(L0_xattn_time_first),
           columns(L1_attn_g_q), columns(L1_attn_g_kv), np.tile(L1_attn_g_head, P // DS)[:, None],
           columns(L1_xattn_bq), L1_xattn_qn_w[:, None], L1_xattn_kn_w[:, None]]
    vec = np.concatenate(vec, 1)
    a["vec"] = np.concatenate([vec, np.zeros((P, 64 - vec.shape[1]), f)], 1)

    w = np.stack([L0_attn_W_Q, L0_attn_W_K, L0_attn_W_V])
    w = w.reshape(3, NHG, HG, KT, P, DH).transpose(4, 1, 0, 3, 2, 5)
    a["wqkv0"] = w.reshape(P, NHG, 3 * KT * HG * DH)
    a["wo0"] = L0_attn_W_O.reshape(NHG, HG, DH, D).transpose(2, 0, 1, 3)
    a["bv0"] = L0_attn_b_V.reshape(-1)
    a["bo0"] = L0_attn_b_O

    def hidden(w, shared):
        w = np.concatenate([w.transpose(1, 0, 2).reshape(D, E * EI), shared], 1)
        return np.concatenate([w, np.zeros((D, NJ * P - HID), f)], 1).reshape(KT, P, NJ, P)
    gate, up = hidden(L0_ffn_w_gate, L0_ffn_sh_gate), hidden(L0_ffn_w_up, L0_ffn_sh_up)
    down = np.concatenate([L0_ffn_w_down.reshape(E * EI, D), L0_ffn_sh_down, np.zeros((NJ * P - HID, D), f)])
    moe = np.concatenate([gate.transpose(1, 2, 0, 3).reshape(P, NJ, D), up.transpose(1, 2, 0, 3).reshape(P, NJ, D),
                          down.reshape(NJ, P, D).transpose(1, 0, 2)], 2)
    a["moe"] = moe
    r = np.concatenate([L0_ffn_router_w.T, L0_ffn_sh_gate_w, np.zeros((D, P - CW), f)], 1)
    a["router"] = r.reshape(KT, P, P).transpose(1, 0, 2)
    owner = np.minimum(np.arange(NJ * P) // EI, E)
    one = (owner[None, :] == np.arange(CW)[:, None]).astype(f)
    a["sel"] = np.concatenate([one] * NSPLIT + [np.zeros((P - NSPLIT * CW, NJ * P), f)]).astype(bf)

    w = np.concatenate([L1_attn_Wq, L1_attn_Wkv], 1)
    a["wqkv1"] = w.reshape(KT, P, 3 * D).transpose(1, 0, 2)
    a["wo1"] = L1_attn_Wo.reshape(KT, P, D).transpose(1, 0, 2)
    a["bqkv1"] = np.concatenate([L1_attn_bq, L1_attn_bkv])
    a["bo1"] = L1_attn_bo
    a["mask8"] = (np.arange(P)[:, None] // DS == np.arange(8)[None, :]).astype(f)

    a["wkvx"] = np.concatenate([L1_xattn_Wk, L1_xattn_Wv], 1).reshape(KT, P, 2 * 512).transpose(1, 0, 2)
    a["bkvx"] = np.concatenate([L1_xattn_bk, L1_xattn_bv])
    a["wqx"] = L1_xattn_Wq.reshape(KT, P, NHG, HG * DH).transpose(1, 2, 0, 3)
    a["wox"] = L1_xattn_Wo.reshape(NHG, HG, DH, D).transpose(2, 0, 1, 3)

    gu = np.stack([L1_ffn_w_gate, L1_ffn_w_up])
    a["bitgu"] = gu.reshape(2, BI, KT, P).transpose(3, 0, 2, 1).reshape(P, 2 * KT * BI)
    dn = np.concatenate([L1_ffn_w_down.T, np.zeros((BJ * P - BI, D), f)])
    a["bitdn"] = dn.reshape(BJ, P, D).transpose(1, 0, 2).reshape(P, BJ * D)
    return {k: np.ascontiguousarray(v) for k, v in a.items()}


def program(nc, arrays, phases=6):
    io = {n: nc.dram_tensor(f"in_{n}", v.shape, mybir.dt.from_np(v.dtype), kind="ExternalInput").ap()
          for n, v in arrays.items()}
    out = nc.dram_tensor("out_x", (P, B, D), F32, kind="ExternalOutput").ap()
    build(nc, io, out, phases)


def kernel(**inputs):
    import concourse.bacc as bacc
    from concourse.bass_utils import run_bass_kernel_spmd

    arrays = layouts(**{k: np.asarray(v) for k, v in inputs.items()})
    nc = bacc.Bacc("TRN2", target_bir_lowering=False, num_devices=1)
    program(nc, arrays)
    r = run_bass_kernel_spmd(nc, [{f"in_{n}": v for n, v in arrays.items()}], core_ids=[0])
    return np.ascontiguousarray(r.results[0]["out_x"].transpose(1, 0, 2))
```
